# Optimizing a Trainium2 kernel written in Bass

```python
import numpy as np
import jax
import jax.numpy as jnp

def _softmax(x, axis=-1):
    return jax.nn.softmax(x, axis=axis)

def _gelu(x):
    return jax.nn.gelu(x, approximate=True)

def _silu(x):
    return jax.nn.silu(x)

def _sigmoid(x):
    return jax.nn.sigmoid(x)

def _layernorm(x, axis=-1, eps=1e-05):
    m = jnp.mean(x, axis=axis, keepdims=True)
    v = jnp.var(x, axis=axis, keepdims=True)
    return (x - m) / jnp.sqrt(v + eps)

def _scatter_add(tgt, idx, src, axis=0):
    return tgt.at[idx].add(src)

def _segment_sum(src, seg, n):
    return jax.ops.segment_sum(src, seg, n)
kernel_name = 'mk_adj_ffn_d1_adj_r2_300630'

def setup_inputs(seed: int=0):
    np.random.seed(seed)
    _w = jnp.asarray

    def _rec_inputs():
        import jax
        import jax.numpy as jnp
        _gk = jax.random.key(seed)
        x = -0.0002928 + 1 * jax.random.normal(jax.random.fold_in(_gk, 1), (64, 128, 128), jnp.float32)
        _a = jax.random.bernoulli(jax.random.fold_in(_gk, 2), 0.0625, (64, 128, 128))
        adj = _a.astype(jnp.int32)
        return (x, adj)
    x, adj = _rec_inputs()

    def _L0_gnn_setup():
        import jax, jax.numpy as jnp
        import numpy as np
        NEG_INF = -9000000000000000.0
        ALPHA = 0.2
        key = jax.random.key(seed)
        k1, k2, k3, k4 = jax.random.split(key, 4)
        B, N, Fin, Fout = (8, 1024, 128, 128)
        h = jax.random.normal(k1, (B, N, Fin), dtype=jnp.float32)
        adj = jax.random.randint(k2, (B, N, N), 0, 2, dtype=jnp.int32)
        W = jax.random.normal(k3, (Fin, Fout), dtype=jnp.float32) * 0.05
        a = jax.random.normal(k4, (2 * Fout, 1), dtype=jnp.float32) * 0.05
        return {'h': h, 'adj': adj, 'W': W, 'a': a}
    _L0_gnn_all = _L0_gnn_setup()
    _L0_gnn_in = {k: v for k, v in _L0_gnn_all.items() if k in ('W', 'a')}
    del _L0_gnn_all

    def _L0_ffn_setup():
        import jax, jax.numpy as jnp
        import numpy as np
        B, T, D, H, E = (16, 2048, 128, 256, 8)
        key = jax.random.key(seed)
        ks = jax.random.split(key, 5)
        x = jax.random.normal(ks[0], (B, T, D), dtype=jnp.float32)
        gate_w = jax.random.normal(ks[1], (D, E), dtype=jnp.float32) * 0.02
        gate_b = jnp.zeros((E,), dtype=jnp.float32)
        W1 = jax.random.normal(ks[2], (E, D, H), dtype=jnp.float32) * 0.02
        b1 = jnp.zeros((E, H), dtype=jnp.float32)
        W2 = jax.random.normal(ks[3], (E, H, D), dtype=jnp.float32) * 0.02
        b2 = jnp.zeros((E, D), dtype=jnp.float32)
        return {'x': x, 'gate_w': gate_w, 'gate_b': gate_b, 'W1': W1, 'b1': b1, 'W2': W2, 'b2': b2}
    _L0_ffn_all = _L0_ffn_setup()
    _L0_ffn_in = {k: v for k, v in _L0_ffn_all.items() if k in ('gate_w', 'gate_b', 'W1', 'b1', 'W2', 'b2')}
    del _L0_ffn_all
    return {'x': x, 'adj': adj, 'L0_gnn_W': _L0_gnn_in['W'], 'L0_gnn_a': _L0_gnn_in['a'], 'L0_ffn_gate_w': _L0_ffn_in['gate_w'], 'L0_ffn_gate_b': _L0_ffn_in['gate_b'], 'L0_ffn_W1': _L0_ffn_in['W1'], 'L0_ffn_b1': _L0_ffn_in['b1'], 'L0_ffn_W2': _L0_ffn_in['W2'], 'L0_ffn_b2': _L0_ffn_in['b2']}

def reference(x, adj, L0_gnn_W, L0_gnn_a, L0_ffn_gate_w, L0_ffn_gate_b, L0_ffn_W1, L0_ffn_b1, L0_ffn_W2, L0_ffn_b2):
    import jax
    import jax.numpy as jnp

    def _L0_gnn_ref(h, adj, W, a):
        import jax, jax.numpy as jnp
        import numpy as np
        NEG_INF = -9000000000000000.0
        ALPHA = 0.2
        Fout = W.shape[1]
        Wh = jnp.matmul(h, W)
        a1 = a[:Fout, 0]
        a2 = a[Fout:, 0]
        s1 = jnp.einsum('bnf,f->bn', Wh, a1)
        s2 = jnp.einsum('bnf,f->bn', Wh, a2)
        e = jax.nn.leaky_relu(s1[:, :, None] + s2[:, None, :], negative_slope=ALPHA)
        attn = jnp.where(adj > 0, e, NEG_INF)
        attn = jax.nn.softmax(attn, axis=2)
        h_prime = jnp.matmul(attn, Wh)
        return h_prime

    def _L0_ffn_ref(x, gate_w, gate_b, W1, b1, W2, b2):
        import jax, jax.numpy as jnp
        import numpy as np
        B, T, D, H, E = (16, 2048, 128, 256, 8)
        Bb, Tt, Dd = x.shape
        Ee = gate_w.shape[1]
        xf = x.reshape(-1, Dd)
        N = xf.shape[0]
        logits = xf @ gate_w + gate_b
        probs = jax.nn.softmax(logits, axis=-1)
        top2_vals, top2_idx = jax.lax.top_k(probs, 2)
        cw = jnp.zeros((N, Ee), dtype=xf.dtype).at[jnp.arange(N)[:, None], top2_idx].add(top2_vals)

        def step(acc, params):
            w1, bb1, w2, bb2, we = params
            h = jax.nn.gelu(xf @ w1 + bb1, approximate=False)
            y = h @ w2 + bb2
            return (acc + we[:, None] * y, None)
        out, _ = jax.lax.scan(step, jnp.zeros_like(xf), (W1, b1, W2, b2, cw.T))
        return out.reshape(Bb, Tt, Dd)
    x = x + _L0_gnn_ref(_layernorm(x, axis=-1), adj, L0_gnn_W, L0_gnn_a)
    x = x + _L0_ffn_ref(_layernorm(x, axis=-1), L0_ffn_gate_w, L0_ffn_gate_b, L0_ffn_W1, L0_ffn_b1, L0_ffn_W2, L0_ffn_b2)
    return x

_drawn_inputs = setup_inputs


def setup_inputs(seed=0):
    import zlib

    import numpy as np

    out = dict(_drawn_inputs(seed))
    spreads = {'L0_ffn_gate_b': (0.0, 0.49), 'L0_ffn_b1': (0.0, 0.8), 'L0_ffn_b2': (0.0, 0.365)}
    factors = {'L0_ffn_gate_w': 2.783, 'L0_ffn_W1': 6.515, 'L0_ffn_W2': 5.918}
    for name, (base, spread) in spreads.items():
        noise = np.random.default_rng([zlib.crc32(name.encode()), seed]).standard_normal(out[name].shape)
        drawn = base * np.exp(spread * noise) if base else spread * noise
        out[name] = jnp.asarray(drawn.astype(out[name].dtype))
    for name, factor in factors.items():
        out[name] = (out[name] * factor).astype(out[name].dtype)
    return out
```

```python
from contextlib import ExitStack

import concourse.bass as bass
from concourse import mybir

F32 = mybir.dt.float32
F32R = mybir.dt.float32r
BF16 = mybir.dt.bfloat16
I32 = mybir.dt.int32
ALU = mybir.AluOpType
ACT = mybir.ActivationFunctionType
AX_X = mybir.AxisListType.X

P = 128
GB = 8
T = GB * P
HT = 512
E = 8
HC = 2
UNITS = E * HC
LAG = 3
RING = 4
MASKED = -9.0e15
SLOPE = 0.2
EPS = 1e-5


class Group:

    def __init__(self, base, reg=None):
        self.base, self.reg = base, reg

    def plus(self, n):
        return Group(self.base + n, self.reg)

    def count(self, per_group, extra):
        c = per_group * self.base + extra
        return c if self.reg is None else self.reg * (2 * per_group) + c

    def least(self, per_group, extra):
        return per_group * self.base + extra

    @property
    def index(self):
        return self.count(1, 0)

    @property
    def parity(self):
        return self.base % 2


def run_iterations(engine, groups, iteration):
    iteration(Group(0), 0)
    iteration(Group(1), 1)
    with engine.Fori(0, (groups - 2) // 2) as reg:
        iteration(Group(2, reg), 2)
        iteration(Group(3, reg), 3)
    iteration(Group(groups), groups)
    iteration(Group(groups + 1), groups + 1)


def build(nc, x, adj, W, a, gate_w, gate_b, W1, b1, W2, b2, out, cw_dram):
    NG = x.shape[0] // GB

    x_v = x.rearrange("(i g) n d -> i n g d", g=GB)
    adj_v = adj.rearrange("(i g) n m -> i n g m", g=GB)
    out_v = out.rearrange("(i g) n d -> i n g d", g=GB)

    with ExitStack() as ctx:
        def sb(name, shape, dt=F32):
            return ctx.enter_context(nc.sbuf_tensor(name, shape, dt))

        def sem(name):
            return ctx.enter_context(nc.semaphore(name))

        z = ctx.enter_context(nc.psum_tensor("z", [P, 2, T], F32))
        y = ctx.enter_context(nc.psum_tensor("y", [P, T], F32))
        front = ctx.enter_context(nc.psum_tensor("front", [P, T], F32))

        w1_raw = sb("w1_raw", [P, UNITS, P])
        w2_raw = sb("w2_raw", [P, UNITS, P])
        w1_hi = sb("w1_hi", [P, UNITS, P], F32R)
        w1_lo = sb("w1_lo", [P, UNITS, P], F32R)
        w2_hi = sb("w2_hi", [P, UNITS, P], F32R)
        w2_lo = sb("w2_lo", [P, UNITS, P], F32R)
        gw_raw = sb("gw_raw", [P, E])
        gw_hi = sb("gw_hi", [P, E], F32R)
        gw_lo = sb("gw_lo", [P, E], F32R)
        gb_rep = sb("gb_rep", [P, GB, E])
        b1_rows = sb("b1_rows", [UNITS, P])
        b1_cols = sb("b1_cols", [P, UNITS])
        b2_rows = sb("b2_rows", [E, P])
        Wg = sb("Wg", [P, P])
        WgT = sb("WgT", [P, P])
        a_cols = sb("a_cols", [P, 2])
        a_rep = sb("a_rep", [P, 2, P])
        wa_rep = sb("wa_rep", [P, 2, P])
        ident = sb("ident", [P, P])
        ident_bf = sb("ident_bf", [P, P], BF16)
        earlier = sb("earlier", [P, GB, E, E])
        minus_half = sb("minus_half", [P, GB])
        xin = sb("xin", [P, T])
        adj_sb = sb("adj_sb", [P, T], I32)
        mask = sb("mask", [P, T], BF16)
        xn = sb("xn", [P, T])
        hT = sb("hT", [P, T])
        scores = sb("scores", [P, T])
        probs = sb("probs", [P, T])
        probsT = sb("probsT", [P, T])
        Wh = sb("Wh", [P, T])
        bn = sb("bn", [P, GB, 6])
        stat = sb("stat", [P, 7, GB])
        rstd = sb("rstd", [P, GB])
        rowmax = sb("rowmax", [P, 3, GB])
        rowsum = sb("rowsum", [P, GB])
        rowinv = sb("rowinv", [P, GB])
        x1 = sb("x1", [P, 2, T])
        x2T_hi = sb("x2T_hi", [P, 2, T], F32R)
        x2T_lo = sb("x2T_lo", [P, 2, T], F32R)
        logits = sb("logits", [P, GB, E])
        rprob = sb("rprob", [P, GB, E])
        rank = sb("rank", [P, GB, E])
        rsmall = sb("rsmall", [P, 3, GB])
        at_least = sb("at_least", [P, GB, E, E])
        greater = sb("greater", [P, GB, E, E])
        cw = sb("cw", [P, 2 * E, GB])
        cwT = sb("cwT", [P, P])
        cwT_rows = sb("cwT_rows", [E, T])
        cwb = sb("cwb", [P, RING, T])
        hid = sb("hid", [P, 2, T])
        hid_hi = sb("hid_hi", [P, RING, T], F32R)
        hid_lo = sb("hid_lo", [P, RING, T], F32R)
        y_sb = sb("y_sb", [P, T])
        out_sb = sb("out_sb", [P, T])

        small_loaded = sem("small_loaded")
        experts_loaded = sem("experts_loaded")
        x_loaded = sem("x_loaded")
        adj_loaded = sem("adj_loaded")
        cw_stored = sem("cw_stored")
        cwT_loaded = sem("cwT_loaded")
        cwb_loaded = [sem(f"cwb_loaded{k}") for k in range(RING)]
        out_stored = sem("out_stored")
        consts_step = sem("consts_step")
        a_rep_ready = sem("a_rep_ready")
        setup_pe = sem("setup_pe")
        setup_act = sem("setup_act")
        weights_split = sem("weights_split")
        mask_ready = sem("mask_ready")
        ln1_step = sem("ln1_step")
        ln2_step = sem("ln2_step")
        rstd1_ready = sem("rstd1_ready")
        rstd2_ready = sem("rstd2_ready")
        xT_done = sem("xT_done")
        hT_ready = sem("hT_ready")
        scores_done = sem("scores_done")
        scores_copied = sem("scores_copied")
        rowmax_step = sem("rowmax_step")
        lrelu_ready = sem("lrelu_ready")
        exp_ready = sem("exp_ready")
        Wh_done = sem("Wh_done")
        Wh_ready = sem("Wh_ready")
        probsT_done = sem("probsT_done")
        probsT_ready = sem("probsT_ready")
        attn_done = sem("attn_done")
        x1_step = sem("x1_step")
        x2T_done = sem("x2T_done")
        x2hi_ready = sem("x2hi_ready")
        x2lo_ready = sem("x2lo_ready")
        gate_done = sem("gate_done")
        router_step = sem("router_step")
        router_exp = sem("router_exp")
        cwT_done = sem("cwT_done")
        cwT_ready = sem("cwT_ready")
        up_done = sem("up_done")
        gelu_done = sem("gelu_done")
        scaled = sem("scaled")
        hi_done = sem("hi_done")
        lo_vector = sem("lo_vector")
        lo_pool = sem("lo_pool")
        down_done = sem("down_done")
        y_copied = sem("y_copied")
        yT_done = sem("yT_done")
        out_ready = sem("out_ready")

        LN_STEPS = 5
        RM_STEPS = 3
        X1_STEPS = 2
        RT_STEPS = 11
        N_SMALL = 8

        block = ctx.enter_context(nc.Block())

        def unit_before(b, s, back):
            return (b, s - back) if s >= back else (b.plus(-1), s - back + UNITS)

        @block.sync
        def _(sp):
            def load_x(k):
                sp.dma_start(xin[:, :].rearrange("n (g d) -> n g d", g=GB), x_v[k]).then_inc(x_loaded, 16)

            def load_adj(k):
                sp.dma_start(adj_sb[:, :].rearrange("n (g m) -> n g m", g=GB), adj_v[k]).then_inc(adj_loaded, 16)

            load_x(0)
            load_adj(0)
            sp.dma_start(Wg[:, :], W).then_inc(small_loaded, 16)
            for k in range(2):
                sp.dma_start(a_cols[:, k:k + 1], a[k * P:(k + 1) * P, :]).then_inc(small_loaded, 16)
            sp.dma_start(gw_raw[:, :], gate_w).then_inc(small_loaded, 16)
            sp.dma_start(b1_rows[:, :], b1.rearrange("e (c p) -> (e c) p", c=HC)).then_inc(small_loaded, 16)
            sp.dma_start(b2_rows[:, :], b2).then_inc(small_loaded, 16)
            gb_row = gate_b.rearrange("(o e) -> o e", o=1).broadcast_to([P, E])
            for half in range(2):
                sp.dma_start(gb_rep[:, half, :], gb_row).then_inc(small_loaded, 16)
            sp.dma_start(w1_raw[:, :, :].rearrange("p (e c) h -> p e (c h)", e=E),
                         W1.rearrange("e d h -> d e h")).then_inc(experts_loaded, 16)
            sp.dma_start(w2_raw[:, :, :], W2.rearrange("e (c p) d -> p (e c) d", c=HC)).then_inc(experts_loaded, 16)

            def broadcast(b, e):
                if b.least(UNITS, 2 * e - 6) > 0:
                    sp.wait_ge(scaled, b.count(UNITS, 2 * e - 6))
                sp.dma_start(cwb[:, e % RING, :], cw_dram[b.index, e:e + 1, :].broadcast_to([P, T]))\
                    .then_inc(cwb_loaded[e % RING], 16)

            def iteration(i, n):
                b, prev = i.plus(-1), i.plus(-2)
                if 1 <= n <= NG:
                    broadcast(b, 4)
                    broadcast(b, 5)
                if n >= 2:
                    sp.wait_ge(out_ready, prev.count(1, 1))
                    sp.dma_start(out_v[prev.index], out_sb[:, :].rearrange("n (g d) -> n g d", g=GB))\
                        .then_inc(out_stored, 16)
                if 1 <= n <= NG:
                    broadcast(b, 6)
                    broadcast(b, 7)
                if n < NG:
                    k = i.plus(1).index % NG
                    sp.wait_ge(x1_step, i.count(X1_STEPS, X1_STEPS))
                    load_x(k)
                    sp.wait_ge(mask_ready, i.count(1, 1))
                    load_adj(k)
                if n < NG:
                    k = i.index
                    sp.wait_ge(cwT_ready, i.count(1, 1))
                    sp.dma_start(cw_dram[k].rearrange("e (g n) -> (e g) n", g=GB), cwT[0:E * GB, :])\
                        .then_inc(cw_stored, 16)
                    sp.wait_ge(cw_stored, i.count(16, 16))
                    sp.dma_start(cwT_rows[:, :], cw_dram[k]).then_inc(cwT_loaded, 16)
                    broadcast(i, 0)
                    for e in range(1, RING):
                        broadcast(i, e)

            run_iterations(sp, NG, iteration)
            sp.wait_ge(x_loaded, 16 * (NG + 1))
            sp.wait_ge(adj_loaded, 16 * (NG + 1))
            sp.wait_ge(out_stored, 16 * NG)
            sp.wait_ge(cw_stored, 16 * NG)

        @block.gpsimd
        def _(pool):
            nc.gpsimd.memset(ident[:, :], 0.0).then_inc(consts_step, 1)
            nc.gpsimd.memset(earlier[:, :, :, :], 1.0).then_inc(consts_step, 1)
            nc.gpsimd.memset(minus_half[:, :], -0.5).then_inc(consts_step, 1)
            nc.gpsimd.memset(cw[:, :, :], 0.0).then_inc(consts_step, 1)
            pool.wait_ge(consts_step, 4)
            nc.gpsimd.affine_select(out=ident[:, :], in_=ident[:, :], compare_op=ALU.not_equal, fill=1.0, base=0,
                                    pattern=[[-1, P]], channel_multiplier=1).then_inc(consts_step, 1)
            nc.gpsimd.affine_select(out=earlier[:, :, :, :], in_=earlier[:, :, :, :], compare_op=ALU.is_gt, fill=0.0,
                                    base=0, pattern=[[0, GB], [1, E], [-1, E]], channel_multiplier=0)\
                .then_inc(consts_step, 1)
            pool.wait_ge(consts_step, 6)
            nc.gpsimd.tensor_copy(ident_bf[:, :], ident[:, :]).then_inc(consts_step, 1)

            def rstd_of(ready):
                nc.gpsimd.tensor_tensor(rstd[:, :], stat[:, 5, :], minus_half[:, :], ALU.pow).then_inc(ready, 1)

            def rstd_and_mask(i, n):
                pool.wait_ge(adj_loaded, i.count(16, 16))
                if n >= 1:
                    pool.wait_ge(scores_done, i.count(1, 0))
                pool.wait_ge(ln1_step, i.count(LN_STEPS, 4))
                rstd_of(rstd1_ready)
                nc.gpsimd.tensor_scalar(mask[:, :], adj_sb[:, :], 0, MASKED, ALU.is_le, ALU.mult).then_inc(mask_ready, 1)

            def low_part(b, s, n):
                pool.wait_ge(hi_done, b.count(UNITS, s + 1))
                if b.least(UNITS, s - 3) > 0:
                    pool.wait_ge(down_done, b.count(UNITS, s - 3))
                nc.gpsimd.tensor_tensor(hid_lo[:, s % RING, :], hid[:, s % 2, :], hid_hi[:, s % RING, :].bitcast(F32),
                                        ALU.subtract).then_inc(lo_pool, 1)

            rstd_and_mask(Group(0), 0)

            def iteration(i, n):
                for s in range(UNITS):
                    ub, us = unit_before(i.plus(-1), s, 1)
                    if us % 2 == 1 and ((s >= 1 and 1 <= n <= NG) or (s == 0 and n >= 2)):
                        low_part(ub, us, n)
                    if s == 7 and n < NG:
                        pool.wait_ge(ln2_step, i.count(LN_STEPS, 4))
                        rstd_of(rstd2_ready)
                    if s == 13 and n < NG:
                        rstd_and_mask(i.plus(1), n + 1)

            run_iterations(pool, NG, iteration)

        @block.scalar
        def _(act):
            act.wait_ge(setup_pe, 1)
            nc.scalar.activation(WgT[:, :], front[:, 0:P], ACT.Copy).then_inc(setup_act, 1)
            nc.scalar.activation(b1_cols[:, :], front[:, P:P + UNITS], ACT.Copy).then_inc(setup_act, 1)
            act.wait_ge(setup_pe, 2)
            nc.scalar.activation(wa_rep[:, :, :].rearrange("p k j -> p (k j)"), front[:, HT:HT + 2 * P], ACT.Copy)\
                .then_inc(setup_act, 1)

            def gelu(b, s):
                act.wait_ge(up_done, b.count(UNITS, s + 1))
                nc.scalar.activation(z[:, s % 2, :], z[:, s % 2, :], ACT.Gelu, bias=b1_cols[:, s:s + 1])\
                    .then_inc(gelu_done, 1)

            def high_part(b, s):
                act.wait_ge(scaled, b.count(UNITS, s + 1))
                if b.least(UNITS, s - 3) > 0:
                    act.wait_ge(down_done, b.count(UNITS, s - 3))
                nc.scalar.activation(hid_hi[:, s % RING, :], hid[:, s % 2, :], ACT.Copy).then_inc(hi_done, 1)

            def front_step(i, n, s):
                if s == 0:
                    act.wait_ge(xT_done, i.count(1, 1))
                    nc.scalar.activation(hT[:, :], front[:, :], ACT.Copy).then_inc(hT_ready, 1)
                if s == 1:
                    act.wait_ge(scores_done, i.count(1, 1))
                    nc.scalar.activation(scores[:, :], front[:, :], ACT.Copy).then_inc(scores_copied, 1)
                if s == 2:
                    act.wait_ge(lrelu_ready, i.count(1, 1))
                    act.wait_ge(rowmax_step, i.count(RM_STEPS, 3))
                    for g in range(GB):
                        row = probs[:, g * P:(g + 1) * P]
                        last = nc.scalar.activation(row, row, ACT.Exp, bias=rowmax[:, 2, g:g + 1],
                                                    accum_out=rowsum[:, g:g + 1])
                    last.then_inc(exp_ready, 1)
                if s == 3:
                    act.wait_ge(Wh_done, i.count(1, 1))
                    nc.scalar.activation(Wh[:, :], front[:, :], ACT.Copy).then_inc(Wh_ready, 1)
                if s == 5:
                    act.wait_ge(probsT_done, i.count(1, 1))
                    nc.scalar.activation(probsT[:, :], front[:, :], ACT.Copy).then_inc(probsT_ready, 1)
                if s == 9:
                    act.wait_ge(x2T_done, i.count(1, 1))
                    if n >= 2:
                        act.wait_ge(up_done, i.count(UNITS, -UNITS))
                    nc.scalar.activation(x2T_hi[:, i.parity, :], front[:, :], ACT.Copy).then_inc(x2hi_ready, 1)
                if s == 10:
                    act.wait_ge(router_step, i.count(RT_STEPS, 3))
                    nc.scalar.activation(rprob[:, :, :], logits[:, :, :], ACT.Exp).then_inc(router_exp, 1)
                if s == 12:
                    act.wait_ge(cwT_done, i.count(1, 1))
                    if n >= 1:
                        act.wait_ge(cw_stored, i.count(16, 0))
                    nc.scalar.activation(cwT[:, :], front[:, 0:P], ACT.Copy).then_inc(cwT_ready, 1)

            def iteration(i, n):
                b = i.plus(-1)
                for s in range(UNITS):
                    if s == 3 and n >= 2:
                        act.wait_ge(down_done, b.count(UNITS, 0))
                        if n >= 3:
                            act.wait_ge(yT_done, b.count(1, -1))
                        nc.scalar.activation(y_sb[:, :], y[:, :], ACT.Copy).then_inc(y_copied, 1)
                    if (s >= 1 and 1 <= n <= NG) or (s == 0 and n >= 2):
                        high_part(*unit_before(b, s, 1))
                    if 1 <= n <= NG:
                        gelu(b, s)
                    if n < NG:
                        front_step(i, n, s)

            run_iterations(act, NG, iteration)

        @block.vector
        def _(dve):
            def ln_stats(i, src, step):
                for g in range(GB):
                    last = nc.vector.bn_stats(bn[:, g, :], src[:, g * P:(g + 1) * P])
                last.then_inc(step, 1)
                dve.wait_ge(step, i.count(LN_STEPS, 1))
                mean_even, mean_odd = bn[:, :, 1], bn[:, :, 4]
                nc.vector.tensor_tensor(stat[:, 1, :], mean_even, mean_odd, ALU.add)
                nc.vector.tensor_tensor(stat[:, 2, :], mean_even, mean_odd, ALU.subtract)
                nc.vector.tensor_tensor(stat[:, 3, :], bn[:, :, 2], bn[:, :, 5], ALU.add).then_inc(step, 1)
                dve.wait_ge(step, i.count(LN_STEPS, 2))
                nc.vector.tensor_scalar(stat[:, 0, :], stat[:, 1, :], 0.5, None, ALU.mult)
                nc.vector.scalar_tensor_tensor(out=stat[:, 4, :], in0=stat[:, 2, :], scalar=0.25, in1=stat[:, 2, :],
                                               op0=ALU.mult, op1=ALU.mult)
                nc.vector.tensor_scalar(stat[:, 6, :], stat[:, 3, :], 1.0 / P, EPS, ALU.mult, ALU.add).then_inc(step, 1)
                dve.wait_ge(step, i.count(LN_STEPS, 3))
                nc.vector.tensor_tensor(stat[:, 5, :], stat[:, 4, :], stat[:, 6, :], ALU.add).then_inc(step, 1)

            def normalise(i, src, step, ready):
                dve.wait_ge(ready, i.count(1, 1))
                for g in range(GB):
                    last = nc.vector.tensor_scalar(xn[:, g * P:(g + 1) * P], src[:, g * P:(g + 1) * P],
                                                   stat[:, 0, g:g + 1], rstd[:, g:g + 1], ALU.subtract, ALU.mult)
                last.then_inc(step, 1)

            def split(hi, lo, raw, count):
                nc.vector.tensor_copy(hi, raw).then_inc(weights_split, 1)
                dve.wait_ge(weights_split, count)
                nc.vector.tensor_tensor(lo, raw, hi.bitcast(F32), ALU.subtract).then_inc(weights_split, 1)

            def scale(b, s):
                dve.wait_ge(gelu_done, b.count(UNITS, s + 1))
                if s % HC == 0:
                    e = s // HC
                    dve.wait_ge(cwb_loaded[e % RING], b.count(32, 16 * (e // RING + 1)))
                if b.least(UNITS, s - 1) > 0:
                    dve.wait_ge(hi_done, b.count(UNITS, s - 1))
                if s % 2 == 1 and b.least(UNITS // 2, (s - 1) // 2) > 0:
                    dve.wait_ge(lo_pool, b.count(UNITS // 2, (s - 1) // 2))
                nc.vector.tensor_tensor(hid[:, s % 2, :], z[:, s % 2, :], cwb[:, (s // HC) % RING, :], ALU.mult)\
                    .then_inc(scaled, 1)

            def low_part(b, s):
                dve.wait_ge(hi_done, b.count(UNITS, s + 1))
                if b.least(UNITS, s - 3) > 0:
                    dve.wait_ge(down_done, b.count(UNITS, s - 3))
                nc.vector.tensor_tensor(hid_lo[:, s % RING, :], hid[:, s % 2, :], hid_hi[:, s % RING, :].bitcast(F32),
                                        ALU.subtract).then_inc(lo_vector, 1)

            def over_e(t):
                return t[:, :, :, None].broadcast_to([P, GB, E, E])

            def over_other(t):
                return t[:, :, None, :].broadcast_to([P, GB, E, E])

            def front_step(i, n, s):
                if s == 2:
                    dve.wait_ge(scores_copied, i.count(1, 1))
                    nc.vector.tensor_reduce(rowmax[:, 0, :], front[:, :].rearrange("p (g j) -> p g j", g=GB), AX_X, ALU.max)\
                        .then_inc(rowmax_step, 1)
                    nc.vector.scalar_tensor_tensor(out=probs[:, :], in0=scores[:, :], scalar=SLOPE, in1=front[:, :],
                                                   op0=ALU.mult, op1=ALU.max).then_inc(lrelu_ready, 1)
                    dve.wait_ge(rowmax_step, i.count(RM_STEPS, 1))
                    nc.vector.tensor_scalar(rowmax[:, 1, :], rowmax[:, 0, :], -1.0, None, ALU.mult).then_inc(rowmax_step, 1)
                    dve.wait_ge(rowmax_step, i.count(RM_STEPS, 2))
                    nc.vector.scalar_tensor_tensor(out=rowmax[:, 2, :], in0=rowmax[:, 1, :], scalar=SLOPE,
                                                   in1=rowmax[:, 1, :], op0=ALU.mult, op1=ALU.min).then_inc(rowmax_step, 1)
                if s == 6:
                    dve.wait_ge(exp_ready, i.count(1, 1))
                    nc.vector.reciprocal(rowinv[:, :], rowsum[:, :]).then_inc(x1_step, 1)
                    dve.wait_ge(x1_step, i.count(X1_STEPS, 1))
                    dve.wait_ge(attn_done, i.count(1, 1))
                    for g in range(GB):
                        cols = slice(g * P, (g + 1) * P)
                        last = nc.vector.scalar_tensor_tensor(out=x1[:, i.parity, cols], in0=front[:, cols],
                                                              scalar=rowinv[:, g:g + 1], in1=xin[:, cols],
                                                              op0=ALU.mult, op1=ALU.add)
                    last.then_inc(x1_step, 1)
                if s == 7:
                    dve.wait_ge(x1_step, i.count(X1_STEPS, 2))
                    ln_stats(i, x1[:, i.parity, :], ln2_step)
                if s == 8:
                    normalise(i, x1[:, i.parity, :], ln2_step, rstd2_ready)
                if s == 9:
                    dve.wait_ge(x2hi_ready, i.count(1, 1))
                    nc.vector.tensor_tensor(x2T_lo[:, i.parity, :], front[:, :], x2T_hi[:, i.parity, :].bitcast(F32),
                                            ALU.subtract).then_inc(x2lo_ready, 1)
                if s == 10:
                    dve.wait_ge(gate_done, i.count(1, 1))
                    nc.vector.tensor_tensor(rank[:, :, :], front[:, 0:GB * E].rearrange("p (g e) -> p g e", g=GB),
                                            gb_rep[:, :, :], ALU.add).then_inc(router_step, 1)
                    dve.wait_ge(router_step, i.count(RT_STEPS, 1))
                    nc.vector.tensor_reduce(rsmall[:, 0, :], rank[:, :, :], AX_X, ALU.max).then_inc(router_step, 1)
                    dve.wait_ge(router_step, i.count(RT_STEPS, 2))
                    nc.vector.tensor_tensor(logits[:, :, :], rank[:, :, :],
                                            rsmall[:, 0, :, None].broadcast_to([P, GB, E]), ALU.subtract)\
                        .then_inc(router_step, 1)
                if s == 11:
                    dve.wait_ge(router_exp, i.count(1, 1))
                    nc.vector.tensor_reduce(rsmall[:, 1, :], rprob[:, :, :], AX_X, ALU.add).then_inc(router_step, 1)
                    dve.wait_ge(router_step, i.count(RT_STEPS, 4))
                    nc.vector.reciprocal(rsmall[:, 2, :], rsmall[:, 1, :]).then_inc(router_step, 1)
                    dve.wait_ge(router_step, i.count(RT_STEPS, 5))
                    nc.vector.tensor_tensor(logits[:, :, :], rprob[:, :, :],
                                            rsmall[:, 2, :, None].broadcast_to([P, GB, E]), ALU.mult)\
                        .then_inc(router_step, 1)
                    dve.wait_ge(router_step, i.count(RT_STEPS, 6))
                    nc.vector.tensor_tensor(at_least[:, :, :, :], over_other(logits), over_e(logits), ALU.is_ge)
                    nc.vector.tensor_tensor(greater[:, :, :, :], over_other(logits), over_e(logits), ALU.is_gt)\
                        .then_inc(router_step, 1)
                    dve.wait_ge(router_step, i.count(RT_STEPS, 7))
                    nc.vector.tensor_tensor(at_least[:, :, :, :], at_least[:, :, :, :], earlier[:, :, :, :], ALU.mult)\
                        .then_inc(router_step, 1)
                    dve.wait_ge(router_step, i.count(RT_STEPS, 8))
                    nc.vector.tensor_tensor(greater[:, :, :, :], at_least[:, :, :, :], greater[:, :, :, :], ALU.max)\
                        .then_inc(router_step, 1)
                    dve.wait_ge(router_step, i.count(RT_STEPS, 9))
                    nc.vector.tensor_reduce(rank[:, :, :], greater[:, :, :, :], AX_X, ALU.add).then_inc(router_step, 1)
                    dve.wait_ge(router_step, i.count(RT_STEPS, 10))
                    nc.vector.scalar_tensor_tensor(out=cw[:, 0:E, :].rearrange("p e g -> p g e"), in0=rank[:, :, :],
                                                   scalar=1.5, in1=logits[:, :, :], op0=ALU.is_lt, op1=ALU.mult)\
                        .then_inc(router_step, 1)

            def next_stats(i, n):
                dve.wait_ge(x_loaded, i.count(16, 16))
                ln_stats(i, xin[:, :], ln1_step)

            dve.wait_ge(small_loaded, 16 * N_SMALL)
            nc.vector.tensor_copy(a_rep[:, :, :], a_cols[:, :, None].broadcast_to([P, 2, P])).then_inc(a_rep_ready, 1)
            for g in range(2, GB):
                nc.vector.tensor_copy(gb_rep[:, g, :], gb_rep[:, 0, :])
            split(gw_hi[:, :], gw_lo[:, :], gw_raw[:, :], 1)
            next_stats(Group(0), 0)
            dve.wait_ge(consts_step, 7)
            normalise(Group(0), xin[:, :], ln1_step, rstd1_ready)

            def iteration(i, n):
                b, prev = i.plus(-1), i.plus(-2)
                for s in range(UNITS):
                    ub, us = unit_before(b, s, 1)
                    if us % 2 == 0 and 1 <= n <= NG and s >= 1:
                        low_part(ub, us)
                    if 1 <= n <= NG:
                        scale(b, s)
                    if s == 4 and n >= 2:
                        dve.wait_ge(yT_done, prev.count(1, 1))
                        if n >= 3:
                            dve.wait_ge(out_stored, prev.count(16, 0))
                        nc.vector.tensor_tensor(out_sb[:, :], front[:, :], x1[:, i.parity, :], ALU.add)\
                            .then_inc(out_ready, 1)
                    if n < NG:
                        front_step(i, n, s)
                    if n == 0 and s == 5:
                        dve.wait_ge(experts_loaded, 32)
                        split(w1_hi[:, :, :], w1_lo[:, :, :], w1_raw[:, :, :], 3)
                    if n == 0 and s == 12:
                        split(w2_hi[:, :, :], w2_lo[:, :, :], w2_raw[:, :, :], 5)
                    if n < NG:
                        if s == 13:
                            next_stats(i.plus(1), n + 1)
                        if s == 14:
                            normalise(i.plus(1), xin[:, :], ln1_step, rstd1_ready)

            run_iterations(dve, NG, iteration)

        @block.tensor
        def _(pe):
            pe.wait_ge(small_loaded, 16 * N_SMALL)
            pe.wait_ge(consts_step, 7)
            nc.tensor.transpose(front[:, 0:P], Wg[:, :], ident[:, :])
            nc.tensor.transpose(front[:, P:P + UNITS], b1_rows[:, :], ident[0:UNITS, 0:UNITS]).then_inc(setup_pe, 1)
            pe.wait_ge(setup_act, 1)
            pe.wait_ge(a_rep_ready, 1)
            nc.tensor.matmul(front[:, HT:HT + 2 * P], WgT[:, :], a_rep[:, :, :].rearrange("p k j -> p (k j)"),
                             start=True, stop=True).then_inc(setup_pe, 1)

            halves = [slice(k * HT, (k + 1) * HT) for k in range(T // HT)]
            graphs = [slice(g * P, (g + 1) * P) for g in range(GB)]

            def transposes(src):
                for g in graphs:
                    last = nc.tensor.transpose(front[:, g], src[:, g], ident[:, :])
                return last

            def up(b, s, p):
                if b.least(UNITS, s - 1) > 0:
                    pe.wait_ge(scaled, b.count(UNITS, s - 1))
                if s == 0:
                    pe.wait_ge(x2hi_ready, b.count(1, 1))
                    pe.wait_ge(x2lo_ready, b.count(1, 1))
                    pe.wait_ge(weights_split, 4)
                for k, (w, t) in enumerate(((w1_hi, x2T_hi), (w1_hi, x2T_lo), (w1_lo, x2T_hi))):
                    for h in halves:
                        last = nc.tensor.matmul(z[:, s % 2, h], w[:, s, :], t[:, p, h], start=(k == 0), stop=(k == 2))
                last.then_inc(up_done, 1)

            def down(b, s):
                if s == 0:
                    if b.base >= 1:
                        pe.wait_ge(y_copied, b.count(1, 0))
                    pe.wait_ge(cwT_loaded, b.count(16, 16))
                    pe.wait_ge(weights_split, 6)
                    for h in halves:
                        nc.tensor.matmul(y[:, h], b2_rows[:, :], cwT_rows[:, h], start=True, stop=False)
                pe.wait_ge(hi_done, b.count(UNITS, s + 1))
                pe.wait_ge(lo_pool if s % 2 else lo_vector, b.count(UNITS // 2, s // 2 + 1))
                r = s % RING
                for k, (w, t) in enumerate(((w2_hi, hid_hi), (w2_lo, hid_hi), (w2_hi, hid_lo))):
                    for h in halves:
                        last = nc.tensor.matmul(y[:, h], w[:, s, :], t[:, r, h], start=False,
                                                stop=(k == 2 and s == UNITS - 1))
                last.then_inc(down_done, 1)

            def front_step(i, n, s):
                if s == 0:
                    pe.wait_ge(ln1_step, i.count(LN_STEPS, 5))
                    if n >= 1:
                        pe.wait_ge(cwT_ready, i.count(1, 0))
                    else:
                        pe.wait_ge(setup_act, 3)
                    transposes(xn).then_inc(xT_done, 1)
                if s == 1:
                    pe.wait_ge(hT_ready, i.count(1, 1))
                    pe.wait_ge(mask_ready, i.count(1, 1))
                    for h in halves:
                        nc.tensor.matmul(front[:, h], wa_rep[:, 1, :], hT[:, h], start=True, stop=False)
                    for g in graphs:
                        nc.tensor.matmul(front[:, g], hT[:, g], wa_rep[:, 0, :], start=False, stop=False)
                    for h in halves:
                        last = nc.tensor.matmul(front[:, h], ident_bf[:, :], mask[:, h], start=False, stop=True)
                    last.then_inc(scores_done, 1)
                if s == 3:
                    pe.wait_ge(scores_copied, i.count(1, 1))
                    pe.wait_ge(lrelu_ready, i.count(1, 1))
                    for g in graphs:
                        last = nc.tensor.matmul(front[:, g], hT[:, g], Wg[:, :], start=True, stop=True)
                    last.then_inc(Wh_done, 1)
                if s == 5:
                    pe.wait_ge(exp_ready, i.count(1, 1))
                    pe.wait_ge(Wh_ready, i.count(1, 1))
                    if n >= 2:
                        pe.wait_ge(out_ready, i.count(1, -1))
                    transposes(probs).then_inc(probsT_done, 1)
                if s == 6:
                    pe.wait_ge(probsT_ready, i.count(1, 1))
                    for g in graphs:
                        last = nc.tensor.matmul(front[:, g], probsT[:, g], Wh[:, g], start=True, stop=True)
                    last.then_inc(attn_done, 1)
                if s == 9:
                    pe.wait_ge(ln2_step, i.count(LN_STEPS, 5))
                    transposes(xn).then_inc(x2T_done, 1)
                if s == 10:
                    pe.wait_ge(x2hi_ready, i.count(1, 1))
                    pe.wait_ge(x2lo_ready, i.count(1, 1))
                    for n_g, g in enumerate(graphs):
                        o = front[:, n_g * E:(n_g + 1) * E]
                        nc.tensor.matmul(o, x2T_hi[:, i.parity, g], gw_hi[:, :], start=True, stop=False)
                        nc.tensor.matmul(o, x2T_hi[:, i.parity, g], gw_lo[:, :], start=False, stop=False)
                        last = nc.tensor.matmul(o, x2T_lo[:, i.parity, g], gw_hi[:, :], start=False, stop=True)
                    last.then_inc(gate_done, 1)
                if s == 12:
                    pe.wait_ge(router_step, i.count(RT_STEPS, 11))
                    nc.tensor.transpose(front[:, 0:P], cw[:, :, :].rearrange("p e g -> p (e g)"), ident[:, :])\
                        .then_inc(cwT_done, 1)

            def iteration(i, n):
                b, prev = i.plus(-1), i.plus(-2)
                for s in range(UNITS):
                    if n < NG:
                        front_step(i, n, s)
                    if s == 4 and n >= 2:
                        pe.wait_ge(y_copied, prev.count(1, 1))
                        if n < NG:
                            pe.wait_ge(Wh_ready, i.count(1, 1))
                        elif n > NG:
                            pe.wait_ge(out_ready, prev.count(1, 0))
                        transposes(y_sb).then_inc(yT_done, 1)
                    if 1 <= n <= NG:
                        up(b, s, b.parity)
                    if (s >= LAG and 1 <= n <= NG) or (s < LAG and n >= 2):
                        down(*unit_before(b, s, LAG))

            run_iterations(pe, NG, iteration)


_INS = ["x", "adj", "L0_gnn_W", "L0_gnn_a", "L0_ffn_gate_w", "L0_ffn_gate_b", "L0_ffn_W1", "L0_ffn_b1", "L0_ffn_W2",
        "L0_ffn_b2"]


def kernel(**inputs):
    import numpy as np
    import concourse.bacc as bacc
    from concourse.bass_utils import run_bass_kernel_spmd

    nc = bacc.Bacc("TRN2", target_bir_lowering=False, num_devices=1)
    arrays, args = {}, []
    for name in _INS:
        v = np.ascontiguousarray(inputs[name])
        arrays[f"in_{name}"] = v
        args.append(nc.dram_tensor(f"in_{name}", v.shape, mybir.dt.from_np(v.dtype), kind="ExternalInput").ap())
    out = nc.dram_tensor("out_x", inputs["x"].shape, F32, kind="ExternalOutput").ap()
    groups = inputs["x"].shape[0] // GB
    cw_dram = nc.dram_tensor("cw_dram", (groups, E, T), F32, kind="Internal").ap()
    build(nc, *args, out, cw_dram)
    r = run_bass_kernel_spmd(nc, [arrays], core_ids=[0])
    return r.results[0]["out_x"]
```

```python
from contextlib import ExitStack

import concourse.bass as bass
from concourse import mybir

F32 = mybir.dt.float32
F32R = mybir.dt.float32r
BF16 = mybir.dt.bfloat16
I32 = mybir.dt.int32
ALU = mybir.AluOpType
ACT = mybir.ActivationFunctionType
AX_X = mybir.AxisListType.X

P = 128
GB = 8
T = GB * P
HT = 512
E = 8
HC = 2
UNITS = E * HC
LAG = 3
RING = 4
MASKED = -9.0e15
SLOPE = 0.2
EPS = 1e-5


class Group:

    def __init__(self, base, reg=None):
        self.base, self.reg = base, reg

    def plus(self, n):
        return Group(self.base + n, self.reg)

    def count(self, per_group, extra):
        c = per_group * self.base + extra
        return c if self.reg is None else self.reg * (2 * per_group) + c

    def least(self, per_group, extra):
        return per_group * self.base + extra

    @property
    def index(self):
        return self.count(1, 0)

    @property
    def parity(self):
        return self.base % 2


def run_iterations(engine, groups, iteration):
    iteration(Group(-1), -1)
    iteration(Group(0), 0)
    iteration(Group(1), 1)
    with engine.Fori(0, (groups - 2) // 2) as reg:
        iteration(Group(2, reg), 2)
        iteration(Group(3, reg), 3)
    iteration(Group(groups), groups)
    iteration(Group(groups + 1), groups + 1)


def build(nc, x, adj, W, a, gate_w, gate_b, W1, b1, W2, b2, out, cw_dram):
    NG = x.shape[0] // GB

    x_v = x.rearrange("(i g) n d -> i n g d", g=GB)
    adj_v = adj.rearrange("(i g) n m -> i n g m", g=GB)
    out_v = out.rearrange("(i g) n d -> i n g d", g=GB)

    with ExitStack() as ctx:
        def sb(name, shape, dt=F32):
            return ctx.enter_context(nc.sbuf_tensor(name, shape, dt))

        def sem(name):
            return ctx.enter_context(nc.semaphore(name))

        z = ctx.enter_context(nc.psum_tensor("z", [P, 2, T], F32))
        y = ctx.enter_context(nc.psum_tensor("y", [P, T], F32))
        front = ctx.enter_context(nc.psum_tensor("front", [P, T], F32))

        w1_raw = sb("w1_raw", [P, UNITS, P])
        w2_raw = sb("w2_raw", [P, UNITS, P])
        w1_hi = sb("w1_hi", [P, UNITS, P], F32R)
        w1_lo = sb("w1_lo", [P, UNITS, P], F32R)
        w2_hi = sb("w2_hi", [P, UNITS, P], F32R)
        w2_lo = sb("w2_lo", [P, UNITS, P], F32R)
        gw_raw = sb("gw_raw", [P, E])
        gw_parts = sb("gw_parts", [P, 2 * E], F32R)
        gb_rep = sb("gb_rep", [P, GB, E])
        b1_rows = sb("b1_rows", [UNITS, P])
        b1_cols = sb("b1_cols", [P, UNITS])
        b2_rows = sb("b2_rows", [E, P])
        Wg = sb("Wg", [P, P])
        WgT = sb("WgT", [P, P])
        a_cols = sb("a_cols", [P, 2])
        a_rep = sb("a_rep", [P, 2, P])
        wa_rep = sb("wa_rep", [P, 2, P])
        ident = sb("ident", [P, P])
        ident_bf = sb("ident_bf", [P, P], BF16)
        earlier = sb("earlier", [P, GB, E, E])
        minus_half = sb("minus_half", [P, GB])
        xin = sb("xin", [P, 2, T])
        adj_sb = sb("adj_sb", [P, T], I32)
        mask = sb("mask", [P, T], BF16)
        xn1 = sb("xn1", [P, T])
        xn2 = sb("xn2", [P, T])
        hT = sb("hT", [P, T])
        scores = sb("scores", [P, T])
        probs = sb("probs", [P, T])
        probsT = sb("probsT", [P, T])
        Wh = sb("Wh", [P, T])
        bn = sb("bn", [P, GB, 6])
        stat1 = sb("stat1", [P, 7, GB])
        stat2 = sb("stat2", [P, 7, GB])
        rstd1 = sb("rstd1", [P, GB])
        rstd2 = sb("rstd2", [P, GB])
        rowmax = sb("rowmax", [P, 2, GB])
        rowsum = sb("rowsum", [P, GB])
        rowinv = sb("rowinv", [P, GB])
        x1 = sb("x1", [P, 2, T])
        x2T_hi = sb("x2T_hi", [P, 2, T], F32R)
        x2T_lo = sb("x2T_lo", [P, 2, T], F32R)
        logits = sb("logits", [P, GB, E])
        rprob = sb("rprob", [P, GB, E])
        rank = sb("rank", [P, GB, E])
        rsmall = sb("rsmall", [P, 3, GB])
        at_least = sb("at_least", [P, GB, E, E])
        greater = sb("greater", [P, GB, E, E])
        cw = sb("cw", [P, 2 * E, GB])
        cwT = sb("cwT", [P, P])
        cwT_rows = sb("cwT_rows", [E, T])
        cwb = sb("cwb", [P, RING, T])
        hid = sb("hid", [P, 2, T])
        hid_hi = sb("hid_hi", [P, RING, T], F32R)
        hid_lo = sb("hid_lo", [P, RING, T], F32R)
        y_sb = sb("y_sb", [P, T])
        out_sb = sb("out_sb", [P, 2, T])

        small_loaded = sem("small_loaded")
        experts_loaded = sem("experts_loaded")
        x_loaded = sem("x_loaded")
        adj_loaded = sem("adj_loaded")
        cw_stored = sem("cw_stored")
        cwT_loaded = sem("cwT_loaded")
        cwb_loaded = [sem(f"cwb_loaded{k}") for k in range(RING)]
        x1_copied = sem("x1_copied")
        out_stored = sem("out_stored")
        consts_step = sem("consts_step")
        a_rep_ready = sem("a_rep_ready")
        setup_pe = sem("setup_pe")
        setup_act = sem("setup_act")
        weights_split = sem("weights_split")
        mask_ready = sem("mask_ready")
        ln1_step = sem("ln1_step")
        ln2_step = sem("ln2_step")
        rstd1_ready = sem("rstd1_ready")
        rstd2_ready = sem("rstd2_ready")
        xT_done = sem("xT_done")
        hT_ready = sem("hT_ready")
        scores_done = sem("scores_done")
        scores_copied = sem("scores_copied")
        rowmax_step = sem("rowmax_step")
        lrelu_ready = sem("lrelu_ready")
        exp_ready = sem("exp_ready")
        Wh_done = sem("Wh_done")
        Wh_ready = sem("Wh_ready")
        probsT_done = sem("probsT_done")
        probsT_ready = sem("probsT_ready")
        attn_done = sem("attn_done")
        x1_step = sem("x1_step")
        x2T_done = sem("x2T_done")
        x2hi_ready = sem("x2hi_ready")
        x2lo_ready = sem("x2lo_ready")
        gate_done = sem("gate_done")
        router_step = sem("router_step")
        router_exp = sem("router_exp")
        cwT_done = sem("cwT_done")
        cwT_ready = sem("cwT_ready")
        up_done = sem("up_done")
        gelu_done = sem("gelu_done")
        scaled = sem("scaled")
        hi_done = sem("hi_done")
        lo_vector = sem("lo_vector")
        lo_pool = sem("lo_pool")
        down_done = sem("down_done")
        y_copied = sem("y_copied")
        yT_done = sem("yT_done")
        out_ready = sem("out_ready")

        LN_STEPS = 5
        RM_STEPS = 2
        X1_STEPS = 2
        RT_STEPS = 12
        N_SMALL = 8

        block = ctx.enter_context(nc.Block())

        def on_vector(s):
            return s % 4 == 0

        def lows(s):
            return sum(on_vector(k) == on_vector(s) for k in range(s + 1))

        def low_count(b, s):
            on = on_vector(s)
            per_group = sum(on_vector(k) == on for k in range(UNITS))
            return (lo_vector if on else lo_pool), b.count(per_group, lows(s))

        def unit_before(b, s, back):
            return (b, s - back) if s >= back else (b.plus(-1), s - back + UNITS)

        @block.sync
        def _(sp):
            def load_x(k, parity):
                sp.dma_start(xin[:, parity, :].rearrange("n (g d) -> n g d", g=GB), x_v[k]).then_inc(x_loaded, 16)

            def load_adj(k):
                sp.dma_start(adj_sb[:, :].rearrange("n (g m) -> n g m", g=GB), adj_v[k]).then_inc(adj_loaded, 16)

            load_x(0, 0)
            load_adj(0)
            sp.dma_start(Wg[:, :], W).then_inc(small_loaded, 16)
            for k in range(2):
                sp.dma_start(a_cols[:, k:k + 1], a[k * P:(k + 1) * P, :]).then_inc(small_loaded, 16)
            sp.dma_start(gw_raw[:, :], gate_w).then_inc(small_loaded, 16)
            sp.dma_start(b1_rows[:, :], b1.rearrange("e (c p) -> (e c) p", c=HC)).then_inc(small_loaded, 16)
            sp.dma_start(b2_rows[:, :], b2).then_inc(small_loaded, 16)
            gb_row = gate_b.rearrange("(o e) -> o e", o=1).broadcast_to([P, E])
            for half in range(2):
                sp.dma_start(gb_rep[:, half, :], gb_row).then_inc(small_loaded, 16)
            sp.dma_start(w1_raw[:, :, :].rearrange("p (e c) h -> p e (c h)", e=E),
                         W1.rearrange("e d h -> d e h")).then_inc(experts_loaded, 16)
            sp.dma_start(w2_raw[:, :, :], W2.rearrange("e (c p) d -> p (e c) d", c=HC)).then_inc(experts_loaded, 16)

            def broadcast(b, e):
                if b.least(UNITS, 2 * e - 6) > 0:
                    sp.wait_ge(scaled, b.count(UNITS, 2 * e - 6))
                sp.dma_start(cwb[:, e % RING, :], cw_dram[b.index, e:e + 1, :].broadcast_to([P, T]))\
                    .then_inc(cwb_loaded[e % RING], 16)

            def iteration(i, n):
                b, prev = i.plus(-1), i.plus(-2)
                if n < NG:
                    k = i.plus(2).index % NG
                    if n >= 0:
                        sp.wait_ge(x1_step, i.count(X1_STEPS, X1_STEPS))
                    load_x(k, i.parity)
                    sp.wait_ge(mask_ready, i.count(1, 2))
                    load_adj(k)
                if 1 <= n <= NG:
                    if n >= 3:
                        sp.wait_ge(out_stored, i.count(16, -32))
                    sp.dma_start(out_sb[:, b.parity, :], x1[:, b.parity, :]).then_inc(x1_copied, 16)
                if 1 <= n <= NG:
                    broadcast(b, 4)
                    broadcast(b, 5)
                if n >= 2:
                    sp.wait_ge(out_ready, prev.count(1, 1))
                    sp.dma_start(out_v[prev.index], out_sb[:, i.parity, :].rearrange("n (g d) -> n g d", g=GB))\
                        .then_inc(out_stored, 16)
                if 1 <= n <= NG:
                    broadcast(b, 6)
                    broadcast(b, 7)
                if 0 <= n < NG:
                    k = i.index
                    sp.wait_ge(cwT_ready, i.count(1, 1))
                    sp.dma_start(cw_dram[k].rearrange("e (g n) -> (e g) n", g=GB), cwT[0:E * GB, :])\
                        .then_inc(cw_stored, 16)
                    sp.wait_ge(cw_stored, i.count(16, 16))
                    sp.dma_start(cwT_rows[:, :], cw_dram[k]).then_inc(cwT_loaded, 16)
                    broadcast(i, 0)
                    for e in range(1, RING):
                        broadcast(i, e)

            run_iterations(sp, NG, iteration)
            sp.wait_ge(x_loaded, 16 * (NG + 2))
            sp.wait_ge(adj_loaded, 16 * (NG + 2))
            sp.wait_ge(out_stored, 16 * NG)
            sp.wait_ge(x1_copied, 16 * NG)
            sp.wait_ge(cw_stored, 16 * NG)

        @block.gpsimd
        def _(pool):
            nc.gpsimd.memset(ident[:, :], 0.0).then_inc(consts_step, 1)
            nc.gpsimd.memset(earlier[:, :, :, :], 1.0).then_inc(consts_step, 1)
            nc.gpsimd.memset(minus_half[:, :], -0.5).then_inc(consts_step, 1)
            nc.gpsimd.memset(cw[:, :, :], 0.0).then_inc(consts_step, 1)
            pool.wait_ge(consts_step, 4)
            nc.gpsimd.affine_select(out=ident[:, :], in_=ident[:, :], compare_op=ALU.not_equal, fill=1.0, base=0,
                                    pattern=[[-1, P]], channel_multiplier=1).then_inc(consts_step, 1)
            nc.gpsimd.affine_select(out=earlier[:, :, :, :], in_=earlier[:, :, :, :], compare_op=ALU.is_gt, fill=0.0,
                                    base=0, pattern=[[0, GB], [1, E], [-1, E]], channel_multiplier=0)\
                .then_inc(consts_step, 1)
            pool.wait_ge(consts_step, 6)
            nc.gpsimd.tensor_copy(ident_bf[:, :], ident[:, :]).then_inc(consts_step, 1)

            def rstd_of(rstd, stat, ready):
                nc.gpsimd.tensor_tensor(rstd[:, :], stat[:, 5, :], minus_half[:, :], ALU.pow).then_inc(ready, 1)

            def mask_half(h):
                return nc.gpsimd.tensor_scalar(mask[:, h * HT:(h + 1) * HT], adj_sb[:, h * HT:(h + 1) * HT], 0, MASKED,
                                               ALU.is_le, ALU.mult)

            def rstd_and_mask(i):
                pool.wait_ge(adj_loaded, i.count(16, 16))
                if i.base >= 1:
                    pool.wait_ge(scores_done, i.count(1, 0))
                pool.wait_ge(ln1_step, i.count(LN_STEPS, 4))
                rstd_of(rstd1, stat1, rstd1_ready)
                mask_half(0)

            def low_part(b, s, n):
                pool.wait_ge(hi_done, b.count(UNITS, s + 1))
                if b.least(UNITS, s - 3) > 0:
                    pool.wait_ge(down_done, b.count(UNITS, s - 3))
                nc.gpsimd.tensor_tensor(hid_lo[:, s % RING, :], hid[:, s % 2, :], hid_hi[:, s % RING, :].bitcast(F32),
                                        ALU.subtract).then_inc(lo_pool, 1)

            rstd_and_mask(Group(0))
            mask_half(1).then_inc(mask_ready, 1)

            def iteration(i, n):
                for s in range(UNITS):
                    ub, us = unit_before(i.plus(-1), s, 1)
                    if not on_vector(us) and ((s >= 1 and 1 <= n <= NG) or (s == 0 and n >= 2)):
                        low_part(ub, us, n)
                    if s == 9 and n < NG:
                        rstd_and_mask(i.plus(2))
                    if s == 10 and n < NG:
                        mask_half(1).then_inc(mask_ready, 1)
                    if s == 11 and n < NG:
                        pool.wait_ge(ln2_step, i.count(LN_STEPS, LN_STEPS + 4))
                        rstd_of(rstd2, stat2, rstd2_ready)

            run_iterations(pool, NG, iteration)

        @block.scalar
        def _(act):
            act.wait_ge(setup_pe, 1)
            nc.scalar.activation(WgT[:, :], front[:, 0:P], ACT.Copy).then_inc(setup_act, 1)
            nc.scalar.activation(b1_cols[:, :], front[:, P:P + UNITS], ACT.Copy).then_inc(setup_act, 1)
            act.wait_ge(setup_pe, 2)
            nc.scalar.activation(wa_rep[:, :, :].rearrange("p k j -> p (k j)"), front[:, HT:HT + 2 * P], ACT.Copy)\
                .then_inc(setup_act, 1)

            def gelu(b, s):
                act.wait_ge(up_done, b.count(UNITS, s + 1))
                nc.scalar.activation(z[:, s % 2, :], z[:, s % 2, :], ACT.Gelu, bias=b1_cols[:, s:s + 1])\
                    .then_inc(gelu_done, 1)

            def high_part(b, s):
                act.wait_ge(scaled, b.count(UNITS, s + 1))
                if b.least(UNITS, s - 3) > 0:
                    act.wait_ge(down_done, b.count(UNITS, s - 3))
                nc.scalar.activation(hid_hi[:, s % RING, :], hid[:, s % 2, :], ACT.Copy).then_inc(hi_done, 1)

            def router_front(i, n, s):
                if s == 0:
                    act.wait_ge(x2T_done, i.count(1, 1))
                    if n >= 2:
                        act.wait_ge(up_done, i.count(UNITS, -UNITS))
                    nc.scalar.activation(x2T_hi[:, i.parity, :], front[:, :], ACT.Copy).then_inc(x2hi_ready, 1)
                if s == 5:
                    act.wait_ge(router_step, i.count(RT_STEPS, 4))
                    nc.scalar.activation(rprob[:, :, :], logits[:, :, :], ACT.Exp).then_inc(router_exp, 1)
                if s == 11:
                    act.wait_ge(cwT_done, i.count(1, 1))
                    if n >= 1:
                        act.wait_ge(cw_stored, i.count(16, 0))
                    nc.scalar.activation(cwT[:, :], front[:, 0:P], ACT.Copy).then_inc(cwT_ready, 1)

            def attention_front(j, s):
                if s == 1:
                    act.wait_ge(xT_done, j.count(1, 1))
                    nc.scalar.activation(hT[:, :], front[:, :], ACT.Copy).then_inc(hT_ready, 1)
                if s == 3:
                    act.wait_ge(scores_done, j.count(1, 1))
                    nc.scalar.activation(scores[:, :], front[:, :], ACT.Copy).then_inc(scores_copied, 1)
                if s == 5:
                    act.wait_ge(rowmax_step, j.count(RM_STEPS, 2))
                    for g in range(GB):
                        row = probs[:, g * P:(g + 1) * P]
                        last = nc.scalar.activation(row, row, ACT.Exp, bias=rowmax[:, 1, g:g + 1],
                                                    accum_out=rowsum[:, g:g + 1])
                    last.then_inc(exp_ready, 1)
                if s == 6:
                    act.wait_ge(Wh_done, j.count(1, 1))
                    nc.scalar.activation(Wh[:, :], front[:, :], ACT.Copy).then_inc(Wh_ready, 1)
                if s == 8:
                    act.wait_ge(probsT_done, j.count(1, 1))
                    nc.scalar.activation(probsT[:, :], front[:, :], ACT.Copy).then_inc(probsT_ready, 1)

            def iteration(i, n):
                b = i.plus(-1)
                for s in range(UNITS):
                    if s == 3 and n >= 2:
                        act.wait_ge(down_done, b.count(UNITS, 0))
                        if n >= 3:
                            act.wait_ge(yT_done, b.count(1, -1))
                        nc.scalar.activation(y_sb[:, :], y[:, :], ACT.Copy).then_inc(y_copied, 1)
                    if (s >= 1 and 1 <= n <= NG) or (s == 0 and n >= 2):
                        high_part(*unit_before(b, s, 1))
                    if 0 <= n < NG:
                        router_front(i, n, s)
                    if n < NG:
                        attention_front(i.plus(1), s)
                    if 1 <= n <= NG:
                        gelu(b, s)

            run_iterations(act, NG, iteration)

        @block.vector
        def _(dve):
            def ln_stats(i, src, stat, step):
                for g in range(GB):
                    last = nc.vector.bn_stats(bn[:, g, :], src[:, g * P:(g + 1) * P])
                last.then_inc(step, 1)
                dve.wait_ge(step, i.count(LN_STEPS, 1))
                mean_even, mean_odd = bn[:, :, 1], bn[:, :, 4]
                nc.vector.tensor_tensor(stat[:, 1, :], mean_even, mean_odd, ALU.add)
                nc.vector.tensor_tensor(stat[:, 2, :], mean_even, mean_odd, ALU.subtract)
                nc.vector.tensor_tensor(stat[:, 3, :], bn[:, :, 2], bn[:, :, 5], ALU.add).then_inc(step, 1)
                dve.wait_ge(step, i.count(LN_STEPS, 2))
                nc.vector.tensor_scalar(stat[:, 0, :], stat[:, 1, :], 0.5, None, ALU.mult)
                nc.vector.scalar_tensor_tensor(out=stat[:, 4, :], in0=stat[:, 2, :], scalar=0.25, in1=stat[:, 2, :],
                                               op0=ALU.mult, op1=ALU.mult)
                nc.vector.tensor_scalar(stat[:, 6, :], stat[:, 3, :], 1.0 / P, EPS, ALU.mult, ALU.add).then_inc(step, 1)
                dve.wait_ge(step, i.count(LN_STEPS, 3))
                nc.vector.tensor_tensor(stat[:, 5, :], stat[:, 4, :], stat[:, 6, :], ALU.add).then_inc(step, 1)

            def normalise(i, xn, src, stat, rstd, step, ready):
                dve.wait_ge(ready, i.count(1, 1))
                for g in range(GB):
                    last = nc.vector.tensor_scalar(xn[:, g * P:(g + 1) * P], src[:, g * P:(g + 1) * P],
                                                   stat[:, 0, g:g + 1], rstd[:, g:g + 1], ALU.subtract, ALU.mult)
                last.then_inc(step, 1)

            def split(hi, lo, raw, count):
                nc.vector.tensor_copy(hi, raw).then_inc(weights_split, 1)
                dve.wait_ge(weights_split, count)
                nc.vector.tensor_tensor(lo, raw, hi.bitcast(F32), ALU.subtract).then_inc(weights_split, 1)

            def scale(b, s):
                dve.wait_ge(gelu_done, b.count(UNITS, s + 1))
                if s % HC == 0:
                    e = s // HC
                    dve.wait_ge(cwb_loaded[e % RING], b.count(32, 16 * (e // RING + 1)))
                if b.least(UNITS, s - 1) > 0:
                    dve.wait_ge(hi_done, b.count(UNITS, s - 1))
                before, last = unit_before(b, s, 2)
                if not on_vector(last) and before.base >= 0:
                    dve.wait_ge(*low_count(before, last))
                nc.vector.tensor_tensor(hid[:, s % 2, :], z[:, s % 2, :], cwb[:, (s // HC) % RING, :], ALU.mult)\
                    .then_inc(scaled, 1)

            def low_part(b, s):
                dve.wait_ge(hi_done, b.count(UNITS, s + 1))
                if b.least(UNITS, s - 3) > 0:
                    dve.wait_ge(down_done, b.count(UNITS, s - 3))
                nc.vector.tensor_tensor(hid_lo[:, s % RING, :], hid[:, s % 2, :], hid_hi[:, s % RING, :].bitcast(F32),
                                        ALU.subtract).then_inc(lo_vector, 1)

            def over_e(t):
                return t[:, :, :, None].broadcast_to([P, GB, E, E])

            def over_other(t):
                return t[:, :, None, :].broadcast_to([P, GB, E, E])

            def router_front(i, n, s):
                if s == 0:
                    dve.wait_ge(x2hi_ready, i.count(1, 1))
                    nc.vector.tensor_tensor(x2T_lo[:, i.parity, :], front[:, :], x2T_hi[:, i.parity, :].bitcast(F32),
                                            ALU.subtract).then_inc(x2lo_ready, 1)
                if s == 2:
                    dve.wait_ge(gate_done, i.count(1, 1))
                    parts = front[:, 0:GB * 2 * E].rearrange("p (g k e) -> p g k e", g=GB, k=2)
                    nc.vector.tensor_tensor(rank[:, :, :], parts[:, :, 0, :], gb_rep[:, :, :], ALU.add)\
                        .then_inc(router_step, 1)
                    dve.wait_ge(router_step, i.count(RT_STEPS, 1))
                    nc.vector.tensor_tensor(rank[:, :, :], parts[:, :, 1, :], rank[:, :, :], ALU.add)\
                        .then_inc(router_step, 1)
                    dve.wait_ge(router_step, i.count(RT_STEPS, 2))
                    nc.vector.tensor_reduce(rsmall[:, 0, :], rank[:, :, :], AX_X, ALU.max).then_inc(router_step, 1)
                    dve.wait_ge(router_step, i.count(RT_STEPS, 3))
                    nc.vector.tensor_tensor(logits[:, :, :], rank[:, :, :],
                                            rsmall[:, 0, :, None].broadcast_to([P, GB, E]), ALU.subtract)\
                        .then_inc(router_step, 1)
                if s == 6:
                    dve.wait_ge(router_exp, i.count(1, 1))
                    nc.vector.tensor_reduce(rsmall[:, 1, :], rprob[:, :, :], AX_X, ALU.add).then_inc(router_step, 1)
                    dve.wait_ge(router_step, i.count(RT_STEPS, 5))
                    nc.vector.reciprocal(rsmall[:, 2, :], rsmall[:, 1, :]).then_inc(router_step, 1)
                    dve.wait_ge(router_step, i.count(RT_STEPS, 6))
                    nc.vector.tensor_tensor(logits[:, :, :], rprob[:, :, :],
                                            rsmall[:, 2, :, None].broadcast_to([P, GB, E]), ALU.mult)\
                        .then_inc(router_step, 1)
                    dve.wait_ge(router_step, i.count(RT_STEPS, 7))
                    nc.vector.tensor_tensor(at_least[:, :, :, :], over_other(logits), over_e(logits), ALU.is_ge)
                    nc.vector.tensor_tensor(greater[:, :, :, :], over_other(logits), over_e(logits), ALU.is_gt)\
                        .then_inc(router_step, 1)
                if s == 7:
                    dve.wait_ge(router_step, i.count(RT_STEPS, 8))
                    nc.vector.tensor_tensor(at_least[:, :, :, :], at_least[:, :, :, :], earlier[:, :, :, :], ALU.mult)\
                        .then_inc(router_step, 1)
                    dve.wait_ge(router_step, i.count(RT_STEPS, 9))
                    nc.vector.tensor_tensor(greater[:, :, :, :], at_least[:, :, :, :], greater[:, :, :, :], ALU.max)\
                        .then_inc(router_step, 1)
                    dve.wait_ge(router_step, i.count(RT_STEPS, 10))
                    nc.vector.tensor_reduce(rank[:, :, :], greater[:, :, :, :], AX_X, ALU.add).then_inc(router_step, 1)
                    dve.wait_ge(router_step, i.count(RT_STEPS, 11))
                    nc.vector.scalar_tensor_tensor(out=cw[:, 0:E, :].rearrange("p e g -> p g e"), in0=rank[:, :, :],
                                                   scalar=1.5, in1=logits[:, :, :], op0=ALU.is_lt, op1=ALU.mult)\
                        .then_inc(router_step, 1)

            def attention_front(j, s):
                if s == 3:
                    dve.wait_ge(scores_copied, j.count(1, 1))
                    nc.vector.scalar_tensor_tensor(out=probs[:, :], in0=scores[:, :], scalar=SLOPE, in1=front[:, :],
                                                   op0=ALU.mult, op1=ALU.max).then_inc(lrelu_ready, 1)
                if s == 4:
                    dve.wait_ge(lrelu_ready, j.count(1, 1))
                    nc.vector.tensor_reduce(rowmax[:, 0, :], probs[:, :].rearrange("p (g j) -> p g j", g=GB), AX_X,
                                            ALU.max).then_inc(rowmax_step, 1)
                    dve.wait_ge(rowmax_step, j.count(RM_STEPS, 1))
                    nc.vector.tensor_scalar(rowmax[:, 1, :], rowmax[:, 0, :], -1.0, None, ALU.mult).then_inc(rowmax_step, 1)
                if s == 9:
                    dve.wait_ge(exp_ready, j.count(1, 1))
                    nc.vector.reciprocal(rowinv[:, :], rowsum[:, :]).then_inc(x1_step, 1)
                    dve.wait_ge(x1_step, j.count(X1_STEPS, 1))
                    dve.wait_ge(attn_done, j.count(1, 1))
                    if j.base >= 2:
                        dve.wait_ge(x1_copied, j.count(16, -16))
                    for g in range(GB):
                        cols = slice(g * P, (g + 1) * P)
                        last = nc.vector.scalar_tensor_tensor(out=x1[:, j.parity, cols], in0=front[:, cols],
                                                              scalar=rowinv[:, g:g + 1], in1=xin[:, j.parity, cols],
                                                              op0=ALU.mult, op1=ALU.add)
                    last.then_inc(x1_step, 1)
                if s == 10:
                    dve.wait_ge(x1_step, j.count(X1_STEPS, 2))
                    ln_stats(j, x1[:, j.parity, :], stat2, ln2_step)
                if s == 12:
                    normalise(j, xn2, x1[:, j.parity, :], stat2, rstd2, ln2_step, rstd2_ready)

            def next_stats(i):
                dve.wait_ge(x_loaded, i.count(16, 16))
                ln_stats(i, xin[:, i.parity, :], stat1, ln1_step)

            def normalise_next(i):
                normalise(i, xn1, xin[:, i.parity, :], stat1, rstd1, ln1_step, rstd1_ready)

            dve.wait_ge(small_loaded, 16 * N_SMALL)
            nc.vector.tensor_copy(a_rep[:, :, :], a_cols[:, :, None].broadcast_to([P, 2, P])).then_inc(a_rep_ready, 1)
            for g in range(2, GB):
                nc.vector.tensor_copy(gb_rep[:, g, :], gb_rep[:, 0, :])
            split(gw_parts[:, 0:E], gw_parts[:, E:2 * E], gw_raw[:, :], 1)
            next_stats(Group(0))
            dve.wait_ge(consts_step, 7)
            normalise_next(Group(0))

            def iteration(i, n):
                b, prev = i.plus(-1), i.plus(-2)
                for s in range(UNITS):
                    ub, us = unit_before(b, s, 1)
                    if on_vector(us) and 1 <= n <= NG and s >= 1:
                        low_part(ub, us)
                    if s == 5 and n >= 2:
                        dve.wait_ge(yT_done, prev.count(1, 1))
                        dve.wait_ge(x1_copied, prev.count(16, 16))
                        nc.vector.tensor_tensor(out_sb[:, i.parity, :], front[:, :], out_sb[:, i.parity, :], ALU.add)\
                            .then_inc(out_ready, 1)
                    if 0 <= n < NG:
                        router_front(i, n, s)
                    if n < NG:
                        attention_front(i.plus(1), s)
                    if 1 <= n <= NG:
                        scale(b, s)
                    if n == -1 and s == 4:
                        dve.wait_ge(experts_loaded, 32)
                        split(w1_hi[:, :, :], w1_lo[:, :, :], w1_raw[:, :, :], 3)
                    if n == 0 and s == 8:
                        split(w2_hi[:, :, :], w2_lo[:, :, :], w2_raw[:, :, :], 5)
                    if n < NG and s == 8:
                        next_stats(i.plus(2))
                    if n < NG and s == 14:
                        dve.wait_ge(xT_done, i.count(1, 2))
                        normalise_next(i.plus(2))

            run_iterations(dve, NG, iteration)

        @block.tensor
        def _(pe):
            pe.wait_ge(small_loaded, 16 * N_SMALL)
            pe.wait_ge(consts_step, 7)
            nc.tensor.transpose(front[:, 0:P], Wg[:, :], ident[:, :])
            nc.tensor.transpose(front[:, P:P + UNITS], b1_rows[:, :], ident[0:UNITS, 0:UNITS]).then_inc(setup_pe, 1)
            pe.wait_ge(setup_act, 1)
            pe.wait_ge(a_rep_ready, 1)
            nc.tensor.matmul(front[:, HT:HT + 2 * P], WgT[:, :], a_rep[:, :, :].rearrange("p k j -> p (k j)"),
                             start=True, stop=True).then_inc(setup_pe, 1)

            halves = [slice(k * HT, (k + 1) * HT) for k in range(T // HT)]
            graphs = [slice(g * P, (g + 1) * P) for g in range(GB)]

            def transposes(src):
                for g in graphs:
                    last = nc.tensor.transpose(front[:, g], src[:, g], ident[:, :])
                return last

            def up(b, s, p):
                if b.least(UNITS, s - 1) > 0:
                    pe.wait_ge(scaled, b.count(UNITS, s - 1))
                if s == 0:
                    pe.wait_ge(x2hi_ready, b.count(1, 1))
                    pe.wait_ge(x2lo_ready, b.count(1, 1))
                    pe.wait_ge(weights_split, 4)
                for k, (w, t) in enumerate(((w1_hi, x2T_hi), (w1_hi, x2T_lo), (w1_lo, x2T_hi))):
                    for h in halves:
                        last = nc.tensor.matmul(z[:, s % 2, h], w[:, s, :], t[:, p, h], start=(k == 0), stop=(k == 2))
                last.then_inc(up_done, 1)

            def down(b, s):
                if s == 0:
                    if b.base >= 1:
                        pe.wait_ge(y_copied, b.count(1, 0))
                    pe.wait_ge(cwT_loaded, b.count(16, 16))
                    pe.wait_ge(weights_split, 6)
                    for h in halves:
                        nc.tensor.matmul(y[:, h], b2_rows[:, :], cwT_rows[:, h], start=True, stop=False)
                pe.wait_ge(hi_done, b.count(UNITS, s + 1))
                pe.wait_ge(*low_count(b, s))
                r = s % RING
                for k, (w, t) in enumerate(((w2_hi, hid_hi), (w2_lo, hid_hi), (w2_hi, hid_lo))):
                    for h in halves:
                        last = nc.tensor.matmul(y[:, h], w[:, s, :], t[:, r, h], start=False,
                                                stop=(k == 2 and s == UNITS - 1))
                last.then_inc(down_done, 1)

            def router_front(i, n, s):
                if s == 0:
                    pe.wait_ge(ln2_step, i.count(LN_STEPS, 5))
                    if n >= 1:
                        pe.wait_ge(cwT_ready, i.count(1, 0))
                    transposes(xn2).then_inc(x2T_done, 1)
                if s == 2:
                    pe.wait_ge(hT_ready, i.count(1, 2))
                    pe.wait_ge(x2hi_ready, i.count(1, 1))
                    pe.wait_ge(x2lo_ready, i.count(1, 1))
                    for n_g, g in enumerate(graphs):
                        o = n_g * 2 * E
                        nc.tensor.matmul(front[:, o:o + 2 * E], x2T_hi[:, i.parity, g], gw_parts[:, :],
                                         start=True, stop=False)
                        last = nc.tensor.matmul(front[:, o:o + E], x2T_lo[:, i.parity, g], gw_parts[:, 0:E],
                                                start=False, stop=True)
                    last.then_inc(gate_done, 1)
                if s == 11:
                    pe.wait_ge(router_step, i.count(RT_STEPS, 12))
                    pe.wait_ge(x1_step, i.count(X1_STEPS, 2 * X1_STEPS))
                    nc.tensor.transpose(front[:, 0:P], cw[:, :, :].rearrange("p e g -> p (e g)"), ident[:, :])\
                        .then_inc(cwT_done, 1)

            def attention_front(j, n, s):
                if s == 1:
                    pe.wait_ge(ln1_step, j.count(LN_STEPS, 5))
                    if n >= 0:
                        pe.wait_ge(x2hi_ready, j.count(1, 0))
                        pe.wait_ge(x2lo_ready, j.count(1, 0))
                    else:
                        pe.wait_ge(setup_act, 3)
                    transposes(xn1).then_inc(xT_done, 1)
                if s == 3:
                    pe.wait_ge(hT_ready, j.count(1, 1))
                    pe.wait_ge(mask_ready, j.count(1, 1))
                    if n >= 0:
                        pe.wait_ge(router_step, j.count(RT_STEPS, 2 - RT_STEPS))
                    for h in halves:
                        nc.tensor.matmul(front[:, h], wa_rep[:, 1, :], hT[:, h], start=True, stop=False)
                    for g in graphs:
                        nc.tensor.matmul(front[:, g], hT[:, g], wa_rep[:, 0, :], start=False, stop=False)
                    for h in halves:
                        last = nc.tensor.matmul(front[:, h], ident_bf[:, :], mask[:, h], start=False, stop=True)
                    last.then_inc(scores_done, 1)
                if s == 6:
                    pe.wait_ge(lrelu_ready, j.count(1, 1))
                    if n >= 2:
                        pe.wait_ge(out_ready, j.count(1, -2))
                    for g in graphs:
                        last = nc.tensor.matmul(front[:, g], hT[:, g], Wg[:, :], start=True, stop=True)
                    last.then_inc(Wh_done, 1)
                if s == 8:
                    pe.wait_ge(exp_ready, j.count(1, 1))
                    pe.wait_ge(Wh_ready, j.count(1, 1))
                    transposes(probs).then_inc(probsT_done, 1)
                if s == 9:
                    pe.wait_ge(probsT_ready, j.count(1, 1))
                    for g in graphs:
                        last = nc.tensor.matmul(front[:, g], probsT[:, g], Wh[:, g], start=True, stop=True)
                    last.then_inc(attn_done, 1)

            def iteration(i, n):
                b, prev = i.plus(-1), i.plus(-2)
                for s in range(UNITS):
                    if 0 <= n < NG:
                        router_front(i, n, s)
                    if n < NG:
                        attention_front(i.plus(1), n, s)
                    if s == 5 and n >= 2:
                        pe.wait_ge(y_copied, prev.count(1, 1))
                        if n < NG:
                            pe.wait_ge(lrelu_ready, i.count(1, 2))
                        elif n == NG:
                            pe.wait_ge(cwT_ready, NG)
                        else:
                            pe.wait_ge(out_ready, prev.count(1, 0))
                        transposes(y_sb).then_inc(yT_done, 1)
                    if 1 <= n <= NG:
                        up(b, s, b.parity)
                    if (s >= LAG and 1 <= n <= NG) or (s < LAG and n >= 2):
                        down(*unit_before(b, s, LAG))

            run_iterations(pe, NG, iteration)


_INS = ["x", "adj", "L0_gnn_W", "L0_gnn_a", "L0_ffn_gate_w", "L0_ffn_gate_b", "L0_ffn_W1", "L0_ffn_b1", "L0_ffn_W2",
        "L0_ffn_b2"]


def kernel(**inputs):
    import numpy as np
    import concourse.bacc as bacc
    from concourse.bass_utils import run_bass_kernel_spmd

    nc = bacc.Bacc("TRN2", target_bir_lowering=False, num_devices=1)
    arrays, args = {}, []
    for name in _INS:
        v = np.ascontiguousarray(inputs[name])
        arrays[f"in_{name}"] = v
        args.append(nc.dram_tensor(f"in_{name}", v.shape, mybir.dt.from_np(v.dtype), kind="ExternalInput").ap())
    out = nc.dram_tensor("out_x", inputs["x"].shape, F32, kind="ExternalOutput").ap()
    groups = inputs["x"].shape[0] // GB
    cw_dram = nc.dram_tensor("cw_dram", (groups, E, T), F32, kind="Internal").ap()
    build(nc, *args, out, cw_dram)
    r = run_bass_kernel_spmd(nc, [arrays], core_ids=[0])
    return r.results[0]["out_x"]
```

```python
from contextlib import ExitStack

import concourse.bass as bass
from concourse import mybir

F32 = mybir.dt.float32
F32R = mybir.dt.float32r
BF16 = mybir.dt.bfloat16
I32 = mybir.dt.int32
ALU = mybir.AluOpType
ACT = mybir.ActivationFunctionType
AX_X = mybir.AxisListType.X

P = 128
GB = 8
T = GB * P
HT = 512
E = 8
HC = 2
UNITS = E * HC
LAG = 4
RING = 4
B2_ROWS = 64 + E
MASKED = -9.0e15
SLOPE = 0.2
EPS = 1e-5

FIRST_UNIT = 27
PE_AT = dict(xT=(-3, 2), Wh=(0, 0), scores=(2, 0), probsT=(7, 2), attn=(11, 1), x2T=(16, 2), gate=(20, 0),
             cwT=(25, 2), yT=(47, 1))
ACT_AT = dict(hT=(-3, 2), Wh=(-2, 2), scores=(1, 2), exp=(5, 1), probsT=(6, 2), x2hi=(15, 2),
              router_exp=(21, 1), cwT=(26, 0), y=(45, 2))
DVE_AT = dict(bn1=(-14, 0), stats1=(-11, 1), norm1a=(-8, 2), norm1b=(-6, 0), s1=(0, 2), lrelu=(3, 0),
              rowmax=(3, 1), less_max=(3, 2), rowsum=(10, 2), x1a=(11, 0), x1b=(11, 0), bn2=(11, 0),
              stats2=(12, 2), norm2a=(13, 2), norm2b=(14, 1), x2lo=(15, 1), logits=(19, 1), router_sum=(21, 2),
              router_rank=(21, 2), cw_split=(29, 0), out=(46, 0))
POOL_AT = dict(rstd1=(-10, 0), mask0=(-8, 2), mask1=(-7, 2), mask2=(-7, 2), mask3=(-6, 0), rstd2=(12, 2))
SP_AT = dict(load=-16, cw=28, x1_copy=31, out=48)
PE_FIRST = (dict(xT=(0, 0), Wh=(1, 0), scores=(1, 1), probsT=(8, 0), attn=(11, 0), x2T=(16, 2), gate=(17, 0)),
            dict(xT=(-4, 0), Wh=(-3, 1), scores=(-1, 2), probsT=(8, 2), attn=(10, 1)))
ACT_FIRST = (dict(hT=(0, 0), Wh=(0, 1), scores=(3, 0), probsT=(11, 2), x2hi=(17, 0), router_exp=(17, 2)),
             dict(hT=(-4, 0), scores=(-1, 0), exp=(4, 1), probsT=(8, 2)))
DVE_FIRST = (dict(bn1=(-14, 0), stats1=(-9, 0), norm1b=(-9, 0), s1=(2, 0), lrelu=(4, 0), rowmax=(4, 1),
                  less_max=(5, 1), rowsum=(10, 0), x1a=(10, 0), x1b=(12, 0), bn2=(12, 0), stats2=(13, 2),
                  norm2b=(14, 1), x2lo=(16, 0), logits=(17, 1), router_sum=(19, 0), router_rank=(19, 1),
                  cw_split=(28, 2)),
             dict(bn1=(-15, 0), stats1=(-15, 0), norm1a=(-11, 0), norm1b=(-10, 1), s1=(-2, 0), lrelu=(-1, 2),
                  rowmax=(0, 2), less_max=(0, 2), stats2=(12, 0), norm2b=(14, 1), x2lo=(15, 1), cw_split=(28, 0)))
POOL_FIRST = (dict(mask1=(-9, 2), mask2=(-7, 2), mask3=(-6, 0), rstd2=(11, 2)),
              dict(rstd1=(-13, 0), mask0=(-13, 0), mask1=(-13, 0), mask2=(-13, 0), mask3=(-13, 0), rstd2=(12, 2)))
SP_FIRST = (dict(cw=22),
            dict(load=-16, x1_copy=29))
FIRST_UNIT_FIRST = 27
WARM = (dict(scores=12, Wh=5, probsT=20, attn=6, x2T=4, gate=13, cwT=6),
        dict(xT=10, scores=10, Wh=5, probsT=9))
SET_UP_SLOTS = (3, 8, 16)
VECTOR_LOWS = (14,)


class Group:

    def __init__(self, base, reg=None):
        self.base, self.reg = base, reg

    def plus(self, n):
        return Group(self.base + n, self.reg)

    def count(self, per_group, extra):
        c = per_group * self.base + extra
        return c if self.reg is None else self.reg * (2 * per_group) + c

    def least(self, per_group, extra):
        return per_group * self.base + extra

    @property
    def index(self):
        return self.count(1, 0)

    @property
    def parity(self):
        return self.base % 2


def run_iterations(engine, groups, iteration):
    for n in (-1, 0, 1):
        iteration(Group(n))
    with engine.Fori(0, (groups - 4) // 2) as reg:
        iteration(Group(2, reg))
        iteration(Group(3, reg))
    for n in range(groups - 2, groups + 2):
        iteration(Group(n))


def build(nc, x, adj, W, a, gate_w, gate_b, W1, b1, W2, b2, out, cw_dram):
    NG = x.shape[0] // GB

    x_v = x.rearrange("(i g) n d -> i n g d", g=GB)
    adj_v = adj.rearrange("(i g) n m -> i n g m", g=GB)
    out_v = out.rearrange("(i g) n d -> i n g d", g=GB)

    with ExitStack() as ctx:
        def sb(name, shape, dt=F32):
            return ctx.enter_context(nc.sbuf_tensor(name, shape, dt))

        def sem(name):
            return ctx.enter_context(nc.semaphore(name))

        z = ctx.enter_context(nc.psum_tensor("z", [P, 2, T], F32))
        y = ctx.enter_context(nc.psum_tensor("y", [P, T], F32))
        front = ctx.enter_context(nc.psum_tensor("front", [P, T], F32))

        w1_hi = sb("w1_hi", [P, UNITS, P], F32R)
        w1_lo = sb("w1_lo", [P, UNITS, P], F32R)
        w2_hi = sb("w2_hi", [P, UNITS, P], F32R)
        w2_lo = sb("w2_lo", [P, UNITS, P], F32R)
        gw_raw = sb("gw_raw", [P, E])
        gw_parts = sb("gw_parts", [P, 2 * E], F32R)
        gb_rep = sb("gb_rep", [P, GB, E])
        b1_rows = sb("b1_rows", [UNITS, P])
        b1_cols = sb("b1_cols", [P, UNITS])
        b2_rows = sb("b2_rows", [B2_ROWS, P])
        b2_parts = sb("b2_parts", [B2_ROWS, P], F32R)
        Wg = sb("Wg", [P, P])
        WgT = sb("WgT", [P, P])
        a2_col = sb("a2_col", [P, 1])
        s1 = sb("s1", [P, GB])
        a1_row = sb("a1_row", [P, P])
        a2_rep = sb("a2_rep", [P, P])
        wa2_rep = sb("wa2_rep", [P, P])
        ident = sb("ident", [P, P])
        ident_bf = sb("ident_bf", [P, P], BF16)
        zeros_bf = sb("zeros_bf", [P, HT], BF16)
        earlier = sb("earlier", [P, GB, E, E])
        minus_half = sb("minus_half", [P, GB])
        xin = sb("xin", [P, 2, T])
        adj_sb = sb("adj_sb", [P, T], I32)
        mask = sb("mask", [P, T], BF16)
        xn1 = sb("xn1", [P, T])
        xn2 = sb("xn2", [P, T])
        hT = sb("hT", [P, T])
        scores = sb("scores", [P, T])
        probs = sb("probs", [P, T])
        probsT = sb("probsT", [P, T])
        Wh = sb("Wh", [P, T])
        bn1 = sb("bn1", [P, GB, 6])
        bn2 = sb("bn2", [P, GB, 6])
        stat1 = sb("stat1", [P, 7, GB])
        stat2 = sb("stat2", [P, 7, GB])
        rstd1 = sb("rstd1", [P, GB])
        rstd2 = sb("rstd2", [P, GB])
        rowmax = sb("rowmax", [P, GB])
        rowsum = sb("rowsum", [P, GB])
        rowinv = sb("rowinv", [P, GB])
        x1 = sb("x1", [P, 2, T])
        x2T_hi = sb("x2T_hi", [P, 2, T], F32R)
        x2T_lo = sb("x2T_lo", [P, 2, T], F32R)
        logits = sb("logits", [P, GB, E])
        rprob = sb("rprob", [P, GB, E])
        rank = sb("rank", [P, GB, E])
        rsmall = sb("rsmall", [P, 3, GB])
        at_least = sb("at_least", [P, GB, E, E])
        greater = sb("greater", [P, GB, E, E])
        cw = sb("cw", [P, 2 * E, GB])
        cw_hi = sb("cw_hi", [P, E, GB], F32R)
        cwT = sb("cwT", [P, P])
        cwT_rows = sb("cwT_rows", [B2_ROWS, T])
        cwT_parts = sb("cwT_parts", [B2_ROWS, T], F32R)
        cwb = sb("cwb", [P, RING, T])
        hid = sb("hid", [P, RING, T])
        hid_hi = sb("hid_hi", [P, RING, T], F32R)
        hid_lo = sb("hid_lo", [P, RING, T], F32R)
        y_sb = sb("y_sb", [P, T])
        w1_raw = cwb[:, 0:2, :].rearrange("p k (u h) -> p (k u) h", h=P)
        w2_raw = cwb[:, 2:4, :].rearrange("p k (u h) -> p (k u) h", h=P)
        out_sb = sb("out_sb", [P, 2, T])

        small_loaded = sem("small_loaded")
        gnn_loaded = sem("gnn_loaded")
        a1_loaded = sem("a1_loaded")
        w1_loaded = sem("w1_loaded")
        w2_loaded = sem("w2_loaded")
        x_loaded = [sem(f"x_loaded{k}") for k in range(2)]
        adj_loaded = sem("adj_loaded")
        cw_stored = sem("cw_stored")
        cwT_loaded = sem("cwT_loaded")
        cwT_split = sem("cwT_split")
        cwb_loaded = [sem(f"cwb_loaded{k}") for k in range(RING)]
        x1_copied = sem("x1_copied")
        out_stored = sem("out_stored")
        consts_step = sem("consts_step")
        a_rep_ready = sem("a_rep_ready")
        setup_pe = sem("setup_pe")
        setup_act = sem("setup_act")
        weights_split = sem("weights_split")
        w2_split = sem("w2_split")
        mask_ready = sem("mask_ready")
        ln1_step = sem("ln1_step")
        ln2_step = sem("ln2_step")
        rstd1_ready = sem("rstd1_ready")
        rstd2_ready = sem("rstd2_ready")
        xT_done = sem("xT_done")
        hT_ready = sem("hT_ready")
        scores_done = sem("scores_done")
        s1_product = sem("s1_product")
        s1_ready = sem("s1_ready")
        scores_copied = sem("scores_copied")
        rowmax_step = sem("rowmax_step")
        lrelu_ready = sem("lrelu_ready")
        less_max_ready = sem("less_max_ready")
        exp_ready = sem("exp_ready")
        Wh_done = sem("Wh_done")
        Wh_ready = sem("Wh_ready")
        probsT_done = sem("probsT_done")
        probsT_ready = sem("probsT_ready")
        attn_done = sem("attn_done")
        x1_step = sem("x1_step")
        x2T_done = sem("x2T_done")
        x2hi_ready = sem("x2hi_ready")
        x2lo_ready = sem("x2lo_ready")
        gate_done = sem("gate_done")
        router_step = sem("router_step")
        router_exp = sem("router_exp")
        cwT_done = sem("cwT_done")
        cwT_ready = sem("cwT_ready")
        up_done = sem("up_done")
        gelu_done = sem("gelu_done")
        scaled = sem("scaled")
        hi_done = sem("hi_done")
        lo_vector = sem("lo_vector")
        lo_pool = sem("lo_pool")
        down_done = sem("down_done")
        y_copied = sem("y_copied")
        yT_done = sem("yT_done")
        out_ready = sem("out_ready")

        LN_STEPS = 5
        X1_STEPS = 3
        RT_STEPS = 14
        N_SMALL = 7

        block = ctx.enter_context(nc.Block())

        def on_vector(s):
            return s in VECTOR_LOWS

        def lows(s):
            return sum(on_vector(k) == on_vector(s) for k in range(s + 1))

        def low_count(b, s):
            on = on_vector(s)
            per_group = sum(on_vector(k) == on for k in range(UNITS))
            return (lo_vector if on else lo_pool), b.count(per_group, lows(s))

        def real(g):
            return 0 <= g.base < NG

        def group_at(tables, step, i, s, place=0):
            slot, p = tables[0][step]
            if i.reg is None:
                for n, own in enumerate(tables[1]):
                    first_slot, first_p = own.get(step, (slot, p))
                    if first_slot == (i.base + 1 - n) * UNITS + s and first_p == place:
                        return Group(n)
            g = i.plus(1 - slot // UNITS)
            taken = i.reg is None and g.base < 2
            return g if slot % UNITS == s and p == place and real(g) and not taken else None

        def unit_at(i, s, back):
            if i.reg is None:
                u = (i.base + 1) * UNITS + s - back - FIRST_UNIT_FIRST
                if 0 <= u < UNITS:
                    return Group(0), u
            slot = s - back - FIRST_UNIT
            g = i.plus(1 + slot // UNITS)
            return (g, slot % UNITS) if real(g) and g.base != 0 else None

        def unit_before(b, s, back):
            return b.plus((s - back) // UNITS), (s - back) % UNITS

        @block.sync
        def _(sp):
            def load_x(g):
                if g.base >= 2:
                    sp.wait_ge(x1_step, g.count(X1_STEPS, -X1_STEPS))
                sp.dma_start(xin[:, g.parity, :].rearrange("n (g d) -> n g d", g=GB), x_v[g.index])\
                    .then_inc(x_loaded[g.parity], 16)

            def load_adj(g):
                if g.base >= 1:
                    sp.wait_ge(mask_ready, g.count(1, 0))
                sp.dma_start(adj_sb[:, :].rearrange("n (g m) -> n g m", g=GB), adj_v[g.index])\
                    .then_inc(adj_loaded, 16)

            load_x(Group(0))
            sp.dma_start(Wg[:, :], W).then_inc(gnn_loaded, 16)
            sp.dma_start(a2_col[:, :], a[P:2 * P, :]).then_inc(gnn_loaded, 16)
            load_adj(Group(0))
            sp.dma_start(a1_row[:, :], a[0:P, :].rearrange("p o -> o p").broadcast_to([P, P])).then_inc(a1_loaded, 16)
            sp.dma_start(b1_rows[:, :], b1.rearrange("e (c p) -> (e c) p", c=HC)).then_inc(small_loaded, 16)
            sp.dma_start(w1_raw.rearrange("p (e c) h -> p e (c h)", e=E),
                         W1.rearrange("e d h -> d e h")).then_inc(w1_loaded, 16)
            sp.dma_start(gw_raw[:, :], gate_w).then_inc(small_loaded, 16)
            gb_row = gate_b.rearrange("(o e) -> o e", o=1).broadcast_to([P, E])
            for half in range(2):
                sp.dma_start(gb_rep[:, half, :], gb_row).then_inc(small_loaded, 16)
            sp.wait_ge(consts_step, 5)
            for row in (0, 32, 64):
                sp.dma_start(b2_rows[row:row + E, :], b2).then_inc(small_loaded, 16)
            sp.dma_start(w2_raw, W2.rearrange("e (c p) d -> p (e c) d", c=HC)).then_inc(w2_loaded, 16)

            def broadcast(b, e):
                if b.base == 0 and e == 0:
                    sp.wait_ge(weights_split, 6)
                    sp.wait_ge(w2_split, 2)
                if b.least(UNITS, 2 * e - 6) > 0:
                    sp.wait_ge(scaled, b.count(UNITS, 2 * e - 6))
                sp.dma_start(cwb[:, e % RING, :], cw_dram[b.index, e:e + 1, :].broadcast_to([P, T]))\
                    .then_inc(cwb_loaded[e % RING], 16)

            def slots(at, first_unit):
                at = {step: (slot, 0) for step, slot in at.items()}
                if "cw" in at:
                    at.update({f"broadcast{e}": (max(at["cw"][0], first_unit + HC * e - 6), 0) for e in range(E)})
                return at

            SP_TABLES = slots(SP_AT, FIRST_UNIT), (slots(SP_FIRST[0], FIRST_UNIT_FIRST), slots(SP_FIRST[1], FIRST_UNIT))

            def iteration(i):
                for s in range(UNITS):
                    g = group_at(SP_TABLES, "load", i, s)
                    if g and g.base > 0:
                        load_x(g)
                        load_adj(g)
                    if g := group_at(SP_TABLES, "cw", i, s):
                        sp.wait_ge(cwT_ready, g.count(1, 1))
                        sp.dma_start(cw_dram[g.index].rearrange("e (g n) -> (e g) n", g=GB), cwT[:, :])\
                            .then_inc(cw_stored, 16)
                        sp.wait_ge(cw_stored, g.count(16, 16))
                        for row, first in ((0, 0), (32, 0), (64, E)):
                            sp.dma_start(cwT_rows[row:row + E, :], cw_dram[g.index, first:first + E, :])\
                                .then_inc(cwT_loaded, 16)
                    for e in range(E):
                        if g := group_at(SP_TABLES, f"broadcast{e}", i, s):
                            broadcast(g, e)
                    if g := group_at(SP_TABLES, "x1_copy", i, s):
                        if g.reg is None:
                            sp.wait_ge(x1_step, g.count(X1_STEPS, X1_STEPS))
                        if g.base >= 2:
                            sp.wait_ge(out_stored, g.count(16, -16))
                        sp.dma_start(out_sb[:, g.parity, :], x1[:, g.parity, :]).then_inc(x1_copied, 16)
                    if g := group_at(SP_TABLES, "out", i, s):
                        sp.wait_ge(out_ready, g.count(1, 1))
                        sp.dma_start(out_v[g.index], out_sb[:, g.parity, :].rearrange("n (g d) -> n g d", g=GB))\
                            .then_inc(out_stored, 16)

            run_iterations(sp, NG, iteration)
            sp.wait_ge(out_stored, 16 * NG)
            sp.wait_ge(x1_copied, 16 * NG)
            sp.wait_ge(cw_stored, 16 * NG)

        @block.gpsimd
        def _(pool):
            nc.gpsimd.memset(zeros_bf[:, :], 0.0)
            nc.gpsimd.memset(ident[:, :], 0.0).then_inc(consts_step, 1)
            nc.gpsimd.memset(earlier[:, :, :, :], 1.0).then_inc(consts_step, 1)
            nc.gpsimd.memset(minus_half[:, :], -0.5).then_inc(consts_step, 1)
            nc.gpsimd.memset(b2_rows[:, :], 0.0).then_inc(consts_step, 1)
            nc.gpsimd.memset(cwT_rows[:, :], 0.0).then_inc(consts_step, 1)
            pool.wait_ge(consts_step, 5)
            nc.gpsimd.affine_select(out=ident[:, :], in_=ident[:, :], compare_op=ALU.not_equal, fill=1.0, base=0,
                                    pattern=[[-1, P]], channel_multiplier=1).then_inc(consts_step, 1)
            nc.gpsimd.affine_select(out=earlier[:, :, :, :], in_=earlier[:, :, :, :], compare_op=ALU.is_gt, fill=0.0,
                                    base=0, pattern=[[0, GB], [1, E], [-1, E]], channel_multiplier=0)\
                .then_inc(consts_step, 1)
            pool.wait_ge(consts_step, 7)
            nc.gpsimd.tensor_copy(ident_bf[:, :], ident[:, :]).then_inc(consts_step, 1)

            def rstd_of(rstd, stat, ready):
                nc.gpsimd.tensor_tensor(rstd[:, :], stat[:, 5, :], minus_half[:, :], ALU.pow).then_inc(ready, 1)

            def mask_quarter(h):
                w = T // 4
                return nc.gpsimd.tensor_scalar(mask[:, h * w:(h + 1) * w], adj_sb[:, h * w:(h + 1) * w], 0, MASKED,
                                               ALU.is_le, ALU.mult)

            def low_part(b, s):
                pool.wait_ge(hi_done, b.count(UNITS, s + 1))
                if b.least(UNITS, s - 3) > 0:
                    pool.wait_ge(down_done, b.count(UNITS, s - 3))
                nc.gpsimd.tensor_tensor(hid_lo[:, s % RING, :], hid[:, s % RING, :], hid_hi[:, s % RING, :].bitcast(F32),
                                        ALU.subtract).then_inc(lo_pool, 1)

            def front_step(i, s, place):
                def group(step):
                    return group_at((POOL_AT, POOL_FIRST), step, i, s, place)

                if g := group("rstd1"):
                    pool.wait_ge(adj_loaded, g.count(16, 16))
                    if g.base >= 1:
                        pool.wait_ge(scores_done, g.count(1, 0))
                    pool.wait_ge(ln1_step, g.count(LN_STEPS, 4))
                    rstd_of(rstd1, stat1, rstd1_ready)
                for k in range(4):
                    if group(f"mask{k}"):
                        last = mask_quarter(k)
                        if k == 3:
                            last.then_inc(mask_ready, 1)
                if g := group("rstd2"):
                    pool.wait_ge(ln2_step, g.count(LN_STEPS, 4))
                    rstd_of(rstd2, stat2, rstd2_ready)

            pool.wait_ge(ln1_step, 4)
            rstd_of(rstd1, stat1, rstd1_ready)
            pool.wait_ge(adj_loaded, 16)
            for k in range(4):
                last = mask_quarter(k)
            last.then_inc(mask_ready, 1)

            def iteration(i):
                for s in range(UNITS):
                    front_step(i, s, 0)
                    unit = unit_at(i, s, 1)
                    if unit and not on_vector(unit[1]):
                        low_part(*unit)
                    front_step(i, s, 2)
                    if (i.base + 1) * UNITS + s == SET_UP_SLOTS[2]:
                        pool.wait_ge(w2_loaded, 16)
                        nc.gpsimd.tensor_copy(w2_hi[:, :, :], w2_raw).then_inc(w2_split, 1)
                        pool.wait_ge(w2_split, 1)
                        nc.gpsimd.tensor_tensor(w2_lo[:, :, :], w2_raw, w2_hi[:, :, :].bitcast(F32), ALU.subtract)\
                            .then_inc(w2_split, 1)

            run_iterations(pool, NG, iteration)

        @block.scalar
        def _(act):
            act.wait_ge(setup_pe, 1)
            nc.scalar.activation(WgT[:, :], front[:, 0:P], ACT.Copy).then_inc(setup_act, 1)
            act.wait_ge(setup_pe, 2)
            nc.scalar.activation(wa2_rep[:, :], front[:, HT:HT + P], ACT.Copy)\
                .then_inc(setup_act, 1)
            act.wait_ge(setup_pe, 3)
            nc.scalar.activation(b1_cols[:, :], front[:, P:P + UNITS], ACT.Copy).then_inc(setup_act, 1)

            def gelu(b, s):
                act.wait_ge(up_done, b.count(UNITS, s + 1))
                before, last = unit_before(b, s, RING)
                if before.base >= 0:
                    act.wait_ge(*low_count(before, last))
                nc.scalar.activation(hid[:, s % RING, :], z[:, s % 2, :], ACT.Gelu, bias=b1_cols[:, s:s + 1])\
                    .then_inc(gelu_done, 1)

            def high_part(b, s):
                act.wait_ge(scaled, b.count(UNITS, s + 1))
                if b.least(UNITS, s - 3) > 0:
                    act.wait_ge(down_done, b.count(UNITS, s - 3))
                nc.scalar.activation(hid_hi[:, s % RING, :], hid[:, s % RING, :], ACT.Copy).then_inc(hi_done, 1)

            def front_step(i, s, place):
                def group(step):
                    return group_at((ACT_AT, ACT_FIRST), step, i, s, place)

                if g := group("x2hi"):
                    act.wait_ge(x2T_done, g.count(1, 1))
                    if g.base >= 2:
                        act.wait_ge(up_done, g.count(UNITS, -UNITS))
                    nc.scalar.activation(x2T_hi[:, g.parity, :], front[:, :], ACT.Copy).then_inc(x2hi_ready, 1)
                if g := group("hT"):
                    act.wait_ge(xT_done, g.count(1, 1))
                    nc.scalar.activation(hT[:, :], front[:, :], ACT.Copy).then_inc(hT_ready, 1)
                if g := group("scores"):
                    act.wait_ge(s1_ready, g.count(1, 1))
                    act.wait_ge(scores_done, g.count(1, 1))
                    for k in range(GB):
                        cols = slice(k * P, (k + 1) * P)
                        last = nc.scalar.activation(scores[:, cols], front[:, cols], ACT.Identity, bias=s1[:, k:k + 1])
                    last.then_inc(scores_copied, 1)
                if g := group("y"):
                    act.wait_ge(down_done, g.count(UNITS, UNITS))
                    if g.base >= 1:
                        act.wait_ge(yT_done, g.count(1, 0))
                    nc.scalar.activation(y_sb[:, :], y[:, :], ACT.Copy).then_inc(y_copied, 1)
                if g := group("router_exp"):
                    act.wait_ge(router_step, g.count(RT_STEPS, 4))
                    nc.scalar.activation(rprob[:, :, :], logits[:, :, :], ACT.Exp).then_inc(router_exp, 1)
                if g := group("exp"):
                    act.wait_ge(less_max_ready, g.count(1, 1))
                    nc.scalar.activation(probs[:, :], probs[:, :], ACT.Exp).then_inc(exp_ready, 1)
                if g := group("Wh"):
                    act.wait_ge(Wh_done, g.count(1, 1))
                    nc.scalar.activation(Wh[:, :], front[:, :], ACT.Copy).then_inc(Wh_ready, 1)
                if g := group("probsT"):
                    act.wait_ge(probsT_done, g.count(1, 1))
                    nc.scalar.activation(probsT[:, :], front[:, :], ACT.Copy).then_inc(probsT_ready, 1)
                if g := group("cwT"):
                    act.wait_ge(cwT_done, g.count(1, 1))
                    if g.base >= 1:
                        act.wait_ge(cw_stored, g.count(16, 0))
                    nc.scalar.activation(cwT[:, :], front[:, 0:P], ACT.Copy).then_inc(cwT_ready, 1)

            def iteration(i):
                for s in range(UNITS):
                    front_step(i, s, 0)
                    if unit := unit_at(i, s, 0):
                        gelu(*unit)
                    front_step(i, s, 1)
                    if unit := unit_at(i, s, 1):
                        high_part(*unit)
                    front_step(i, s, 2)

            run_iterations(act, NG, iteration)

        @block.vector
        def _(dve):
            def ln_bn(bn, src, step):
                for k in range(GB):
                    last = nc.vector.bn_stats(bn[:, k, :], src[:, k * P:(k + 1) * P])
                last.then_inc(step, 1)

            def ln_stats(i, bn, stat, step):
                dve.wait_ge(step, i.count(LN_STEPS, 1))
                mean_even, mean_odd = bn[:, :, 1], bn[:, :, 4]
                nc.vector.tensor_tensor(stat[:, 1, :], mean_even, mean_odd, ALU.add)
                nc.vector.tensor_tensor(stat[:, 2, :], mean_even, mean_odd, ALU.subtract)
                nc.vector.tensor_tensor(stat[:, 3, :], bn[:, :, 2], bn[:, :, 5], ALU.add).then_inc(step, 1)
                dve.wait_ge(step, i.count(LN_STEPS, 2))
                nc.vector.tensor_scalar(stat[:, 0, :], stat[:, 1, :], 0.5, None, ALU.mult)
                nc.vector.scalar_tensor_tensor(out=stat[:, 4, :], in0=stat[:, 2, :], scalar=0.25, in1=stat[:, 2, :],
                                               op0=ALU.mult, op1=ALU.mult)
                nc.vector.tensor_scalar(stat[:, 6, :], stat[:, 3, :], 1.0 / P, EPS, ALU.mult, ALU.add).then_inc(step, 1)
                dve.wait_ge(step, i.count(LN_STEPS, 3))
                nc.vector.tensor_tensor(stat[:, 5, :], stat[:, 4, :], stat[:, 6, :], ALU.add).then_inc(step, 1)

            def normalise(half, xn, src, stat, rstd):
                for g in range(half * GB // 2, (half + 1) * GB // 2):
                    last = nc.vector.tensor_scalar(xn[:, g * P:(g + 1) * P], src[:, g * P:(g + 1) * P],
                                                   stat[:, 0, g:g + 1], rstd[:, g:g + 1], ALU.subtract, ALU.mult)
                return last

            def split(hi, lo, raw, count):
                nc.vector.tensor_copy(hi, raw).then_inc(weights_split, 1)
                dve.wait_ge(weights_split, count)
                nc.vector.tensor_tensor(lo, raw, hi.bitcast(F32), ALU.subtract).then_inc(weights_split, 1)

            def scale(b, s):
                dve.wait_ge(gelu_done, b.count(UNITS, s + 1))
                if s % HC == 0:
                    e = s // HC
                    dve.wait_ge(cwb_loaded[e % RING], b.count(32, 16 * (e // RING + 1)))
                nc.vector.tensor_tensor(hid[:, s % RING, :], hid[:, s % RING, :], cwb[:, (s // HC) % RING, :], ALU.mult)\
                    .then_inc(scaled, 1)

            def low_part(b, s):
                dve.wait_ge(hi_done, b.count(UNITS, s + 1))
                if b.least(UNITS, s - 3) > 0:
                    dve.wait_ge(down_done, b.count(UNITS, s - 3))
                nc.vector.tensor_tensor(hid_lo[:, s % RING, :], hid[:, s % RING, :], hid_hi[:, s % RING, :].bitcast(F32),
                                        ALU.subtract).then_inc(lo_vector, 1)

            def over_e(t):
                return t[:, :, :, None].broadcast_to([P, GB, E, E])

            def over_other(t):
                return t[:, :, None, :].broadcast_to([P, GB, E, E])

            def by_graph(t):
                return t[:, :].rearrange("p (g j) -> p g j", g=GB)

            def front_step(i, s, place):
                def group(step):
                    return group_at((DVE_AT, DVE_FIRST), step, i, s, place)

                if g := group("x2lo"):
                    dve.wait_ge(x2hi_ready, g.count(1, 1))
                    nc.vector.tensor_tensor(x2T_lo[:, g.parity, :], front[:, :], x2T_hi[:, g.parity, :].bitcast(F32),
                                            ALU.subtract).then_inc(x2lo_ready, 1)
                if g := group("logits"):
                    dve.wait_ge(gate_done, g.count(1, 1))
                    parts = front[:, 0:GB * 2 * E].rearrange("p (g k e) -> p g k e", g=GB, k=2)
                    nc.vector.tensor_tensor(rank[:, :, :], parts[:, :, 0, :], gb_rep[:, :, :], ALU.add)\
                        .then_inc(router_step, 1)
                    dve.wait_ge(router_step, g.count(RT_STEPS, 1))
                    nc.vector.tensor_tensor(rank[:, :, :], parts[:, :, 1, :], rank[:, :, :], ALU.add)\
                        .then_inc(router_step, 1)
                    dve.wait_ge(router_step, g.count(RT_STEPS, 2))
                    nc.vector.tensor_reduce(rsmall[:, 0, :], rank[:, :, :], AX_X, ALU.max).then_inc(router_step, 1)
                    dve.wait_ge(router_step, g.count(RT_STEPS, 3))
                    nc.vector.tensor_tensor(logits[:, :, :], rank[:, :, :],
                                            rsmall[:, 0, :, None].broadcast_to([P, GB, E]), ALU.subtract)\
                        .then_inc(router_step, 1)
                if g := group("s1"):
                    if g.base == 0:
                        dve.wait_ge(a1_loaded, 16)
                    dve.wait_ge(Wh_ready, g.count(1, 1))
                    nc.vector.tensor_tensor(by_graph(scores), by_graph(Wh), a1_row[:, None, :].broadcast_to([P, GB, P]),
                                            ALU.mult).then_inc(s1_product, 1)
                    dve.wait_ge(s1_product, g.count(1, 1))
                    nc.vector.tensor_reduce(s1[:, :], by_graph(scores), AX_X, ALU.add).then_inc(s1_ready, 1)
                if g := group("lrelu"):
                    dve.wait_ge(scores_copied, g.count(1, 1))
                    nc.vector.scalar_tensor_tensor(out=probs[:, :], in0=scores[:, :], scalar=SLOPE, in1=scores[:, :],
                                                   op0=ALU.mult, op1=ALU.max).then_inc(lrelu_ready, 1)
                if g := group("rowmax"):
                    dve.wait_ge(lrelu_ready, g.count(1, 1))
                    nc.vector.tensor_reduce(rowmax[:, :], by_graph(probs), AX_X, ALU.max).then_inc(rowmax_step, 1)
                if g := group("less_max"):
                    dve.wait_ge(rowmax_step, g.count(1, 1))
                    nc.vector.tensor_tensor(by_graph(probs), by_graph(probs),
                                            rowmax[:, :, None].broadcast_to([P, GB, P]), ALU.subtract)\
                        .then_inc(less_max_ready, 1)
                if g := group("router_sum"):
                    dve.wait_ge(router_exp, g.count(1, 1))
                    nc.vector.tensor_reduce(rsmall[:, 1, :], rprob[:, :, :], AX_X, ALU.add).then_inc(router_step, 1)
                    dve.wait_ge(router_step, g.count(RT_STEPS, 5))
                    nc.vector.reciprocal(rsmall[:, 2, :], rsmall[:, 1, :]).then_inc(router_step, 1)
                    dve.wait_ge(router_step, g.count(RT_STEPS, 6))
                    nc.vector.tensor_tensor(logits[:, :, :], rprob[:, :, :],
                                            rsmall[:, 2, :, None].broadcast_to([P, GB, E]), ALU.mult)\
                        .then_inc(router_step, 1)
                    dve.wait_ge(router_step, g.count(RT_STEPS, 7))
                    nc.vector.tensor_tensor(at_least[:, :, :, :], over_other(logits), over_e(logits), ALU.is_ge)
                    nc.vector.tensor_tensor(greater[:, :, :, :], over_other(logits), over_e(logits), ALU.is_gt)\
                        .then_inc(router_step, 1)
                if g := group("router_rank"):
                    dve.wait_ge(router_step, g.count(RT_STEPS, 8))
                    nc.vector.tensor_tensor(at_least[:, :, :, :], at_least[:, :, :, :], earlier[:, :, :, :], ALU.mult)\
                        .then_inc(router_step, 1)
                    dve.wait_ge(router_step, g.count(RT_STEPS, 9))
                    nc.vector.tensor_tensor(greater[:, :, :, :], at_least[:, :, :, :], greater[:, :, :, :], ALU.max)\
                        .then_inc(router_step, 1)
                    dve.wait_ge(router_step, g.count(RT_STEPS, 10))
                    nc.vector.tensor_reduce(rank[:, :, :], greater[:, :, :, :], AX_X, ALU.add).then_inc(router_step, 1)
                    dve.wait_ge(router_step, g.count(RT_STEPS, 11))
                    nc.vector.scalar_tensor_tensor(out=cw[:, 0:E, :].rearrange("p e g -> p g e"), in0=rank[:, :, :],
                                                   scalar=1.5, in1=logits[:, :, :], op0=ALU.is_lt, op1=ALU.mult)\
                        .then_inc(router_step, 1)
                    dve.wait_ge(router_step, g.count(RT_STEPS, 12))
                    nc.vector.tensor_copy(cw_hi[:, :, :], cw[:, 0:E, :]).then_inc(router_step, 1)
                    dve.wait_ge(router_step, g.count(RT_STEPS, 13))
                    nc.vector.tensor_tensor(cw[:, E:2 * E, :], cw[:, 0:E, :], cw_hi[:, :, :].bitcast(F32), ALU.subtract)\
                        .then_inc(router_step, 1)
                if g := group("cw_split"):
                    dve.wait_ge(cwT_loaded, g.count(48, 48))
                    if g.base >= 1:
                        dve.wait_ge(down_done, g.count(UNITS, 1 - UNITS))
                    nc.vector.tensor_copy(cwT_parts[:, :], cwT_rows[:, :]).then_inc(cwT_split, 1)
                if g := group("rowsum"):
                    dve.wait_ge(exp_ready, g.count(1, 1))
                    nc.vector.tensor_reduce(rowsum[:, :], by_graph(probs), AX_X, ALU.add).then_inc(x1_step, 1)
                    dve.wait_ge(x1_step, g.count(X1_STEPS, 1))
                    nc.vector.reciprocal(rowinv[:, :], rowsum[:, :]).then_inc(x1_step, 1)
                if g := group("x1a"):
                    dve.wait_ge(x1_step, g.count(X1_STEPS, 2))
                    dve.wait_ge(attn_done, g.count(1, 1))
                    if g.base >= 2:
                        dve.wait_ge(x1_copied, g.count(16, -16))
                    x1_half(g, 0)
                if g := group("x1b"):
                    x1_half(g, 1).then_inc(x1_step, 1)
                if g := group("bn2"):
                    dve.wait_ge(x1_step, g.count(X1_STEPS, 3))
                    ln_bn(bn2, x1[:, g.parity, :], ln2_step)
                if g := group("stats2"):
                    ln_stats(g, bn2, stat2, ln2_step)
                if g := group("norm2a"):
                    dve.wait_ge(rstd2_ready, g.count(1, 1))
                    if g.base >= 1:
                        dve.wait_ge(x2T_done, g.count(1, 0))
                    normalise(0, xn2, x1[:, g.parity, :], stat2, rstd2)
                if g := group("norm2b"):
                    normalise(1, xn2, x1[:, g.parity, :], stat2, rstd2).then_inc(ln2_step, 1)
                if g := group("out"):
                    dve.wait_ge(yT_done, g.count(1, 1))
                    dve.wait_ge(x1_copied, g.count(16, 16))
                    nc.vector.tensor_tensor(out_sb[:, g.parity, :], front[:, :], out_sb[:, g.parity, :], ALU.add)\
                        .then_inc(out_ready, 1)
                if g := group("bn1"):
                    dve.wait_ge(x_loaded[g.parity], g.count(8, 16 - 8 * g.parity))
                    ln_bn(bn1, xin[:, g.parity, :], ln1_step)
                if g := group("stats1"):
                    ln_stats(g, bn1, stat1, ln1_step)
                if g := group("norm1a"):
                    dve.wait_ge(rstd1_ready, g.count(1, 1))
                    dve.wait_ge(xT_done, g.count(1, 0))
                    normalise(0, xn1, xin[:, g.parity, :], stat1, rstd1)
                if g := group("norm1b"):
                    normalise(1, xn1, xin[:, g.parity, :], stat1, rstd1).then_inc(ln1_step, 1)

            def x1_half(g, half):
                for k in range(half * GB // 2, (half + 1) * GB // 2):
                    cols = slice(k * P, (k + 1) * P)
                    last = nc.vector.scalar_tensor_tensor(out=x1[:, g.parity, cols], in0=front[:, cols],
                                                          scalar=rowinv[:, k:k + 1], in1=xin[:, g.parity, cols],
                                                          op0=ALU.mult, op1=ALU.add)
                return last

            dve.wait_ge(x_loaded[0], 16)
            ln_bn(bn1, xin[:, 0, :], ln1_step)
            ln_stats(Group(0), bn1, stat1, ln1_step)
            dve.wait_ge(gnn_loaded, 32)
            nc.vector.tensor_copy(a2_rep[:, :], a2_col[:, :].broadcast_to([P, P])).then_inc(a_rep_ready, 1)
            dve.wait_ge(rstd1_ready, 1)
            normalise(0, xn1, xin[:, 0, :], stat1, rstd1)
            normalise(1, xn1, xin[:, 0, :], stat1, rstd1).then_inc(ln1_step, 1)

            def set_up_step(n, s):
                if (n + 1) * UNITS + s == SET_UP_SLOTS[0]:
                    dve.wait_ge(w1_loaded, 16)
                    split(w1_hi[:, :, :], w1_lo[:, :, :], w1_raw, 1)
                    dve.wait_ge(small_loaded, 16 * N_SMALL)
                    for g in range(2, GB):
                        nc.vector.tensor_copy(gb_rep[:, g, :], gb_rep[:, 0, :])
                    split(gw_parts[:, 0:E], gw_parts[:, E:2 * E], gw_raw[:, :], 3)
                if (n + 1) * UNITS + s == SET_UP_SLOTS[1]:
                    nc.vector.tensor_copy(b2_parts[:, :], b2_rows[:, :]).then_inc(weights_split, 1)
                    dve.wait_ge(weights_split, 5)
                    nc.vector.tensor_tensor(b2_parts[32:32 + E, :], b2_rows[32:32 + E, :],
                                            b2_parts[32:32 + E, :].bitcast(F32), ALU.subtract)\
                        .then_inc(weights_split, 1)

            def iteration(i):
                for s in range(UNITS):
                    front_step(i, s, 0)
                    if unit := unit_at(i, s, 0):
                        scale(*unit)
                    front_step(i, s, 1)
                    unit = unit_at(i, s, 1)
                    if unit and on_vector(unit[1]):
                        low_part(*unit)
                    front_step(i, s, 2)
                    set_up_step(i.base, s)

            run_iterations(dve, NG, iteration)

        @block.tensor
        def _(pe):
            pe.wait_ge(gnn_loaded, 32)
            pe.wait_ge(consts_step, 8)
            nc.tensor.transpose(front[:, 0:P], Wg[:, :], ident[:, :]).then_inc(setup_pe, 1)
            pe.wait_ge(setup_act, 1)
            pe.wait_ge(a_rep_ready, 1)
            nc.tensor.matmul(front[:, HT:HT + P], WgT[:, :], a2_rep[:, :], start=True, stop=True).then_inc(setup_pe, 1)
            pe.wait_ge(small_loaded, 16 * N_SMALL)
            nc.tensor.transpose(front[:, P:P + UNITS], b1_rows[:, :], ident[0:UNITS, 0:UNITS]).then_inc(setup_pe, 1)

            halves = [slice(k * HT, (k + 1) * HT) for k in range(T // HT)]
            graphs = [slice(g * P, (g + 1) * P) for g in range(GB)]

            def transposes(src):
                for g in graphs:
                    last = nc.tensor.transpose(front[:, g], src[:, g], ident[:, :])
                return last

            def up(b, s, p):
                if b.least(UNITS, s - 1) > 0:
                    pe.wait_ge(gelu_done, b.count(UNITS, s - 1))
                if s == 0:
                    pe.wait_ge(x2hi_ready, b.count(1, 1))
                    pe.wait_ge(x2lo_ready, b.count(1, 1))
                    pe.wait_ge(weights_split, 4)
                for k, (w, t) in enumerate(((w1_hi, x2T_hi), (w1_hi, x2T_lo), (w1_lo, x2T_hi))):
                    for h in halves:
                        last = nc.tensor.matmul(z[:, s % 2, h], w[:, s, :], t[:, p, h], start=(k == 0), stop=(k == 2))
                last.then_inc(up_done, 1)

            def down(b, s):
                if s == 0:
                    if b.base >= 1:
                        pe.wait_ge(y_copied, b.count(1, 0))
                    pe.wait_ge(cwT_split, b.count(1, 1))
                    pe.wait_ge(weights_split, 6)
                    pe.wait_ge(w2_split, 2)
                    for h in halves:
                        nc.tensor.matmul(y[:, h], b2_parts[:, :], cwT_parts[:, h], start=True, stop=False)
                pe.wait_ge(hi_done, b.count(UNITS, s + 1))
                pe.wait_ge(*low_count(b, s))
                r = s % RING
                for k, (w, t) in enumerate(((w2_hi, hid_hi), (w2_lo, hid_hi), (w2_hi, hid_lo))):
                    for h in halves:
                        last = nc.tensor.matmul(y[:, h], w[:, s, :], t[:, r, h], start=False,
                                                stop=(k == 2 and s == UNITS - 1))
                last.then_inc(down_done, 1)

            def front_read(step, g):
                return dict(xT=(hT_ready, g.count(1, 1)), scores=(scores_copied, g.count(1, 1)),
                            Wh=(Wh_ready, g.count(1, 1)), probsT=(probsT_ready, g.count(1, 1)),
                            attn=(x1_step, g.count(X1_STEPS, X1_STEPS)), x2T=(x2lo_ready, g.count(1, 1)),
                            gate=(router_step, g.count(RT_STEPS, 2)), cwT=(cwT_ready, g.count(1, 1)),
                            yT=(out_ready, g.count(1, 1)))[step]

            def wait_for_front(step, g):
                def place_of(name, group):
                    slot, place = (PE_FIRST[group.base] if group.base < 2 and group.reg is None else {}).get(name, PE_AT[name])
                    return (group.base * UNITS + slot) * 3 + place
                own = place_of(step, g)
                others = [(place_of(name, g.plus(k)), name, k) for name in PE_AT for k in range(-4, 5) if real(g.plus(k))]
                assert [place for place, _, _ in others].count(own) == 1
                before = [other for other in others if other[0] < own]
                if before:
                    _, name, k = max(before)
                    pe.wait_ge(*front_read(name, g.plus(k)))
                    return
                pe.wait_ge(setup_act, 3)

            def front_step(i, s, place):
                def group(step):
                    g = group_at((PE_AT, PE_FIRST), step, i, s, place)
                    if g:
                        if g.base < 2 and (i.base + 1) * UNITS + s < FIRST_UNIT_FIRST + LAG:
                            for _ in range(WARM[g.base].get(step, 0)):
                                nc.tensor.matmul(y[:, 0:HT], zeros_bf[:, 0:P], zeros_bf[:, :], start=True, stop=True)
                        wait_for_front(step, g)
                    return g

                if g := group("x2T"):
                    pe.wait_ge(ln2_step, g.count(LN_STEPS, 5))
                    transposes(xn2).then_inc(x2T_done, 1)
                if g := group("xT"):
                    pe.wait_ge(ln1_step, g.count(LN_STEPS, 5))
                    transposes(xn1).then_inc(xT_done, 1)
                if g := group("gate"):
                    pe.wait_ge(x2hi_ready, g.count(1, 1))
                    pe.wait_ge(x2lo_ready, g.count(1, 1))
                    if g.base == 0:
                        pe.wait_ge(weights_split, 4)
                    for k, cols in enumerate(graphs):
                        o = k * 2 * E
                        nc.tensor.matmul(front[:, o:o + 2 * E], x2T_hi[:, g.parity, cols], gw_parts[:, :],
                                         start=True, stop=False)
                        last = nc.tensor.matmul(front[:, o:o + E], x2T_lo[:, g.parity, cols], gw_parts[:, 0:E],
                                                start=False, stop=True)
                    last.then_inc(gate_done, 1)
                if g := group("scores"):
                    pe.wait_ge(hT_ready, g.count(1, 1))
                    pe.wait_ge(mask_ready, g.count(1, 1))
                    for h in halves:
                        nc.tensor.matmul(front[:, h], wa2_rep[:, :], hT[:, h], start=True, stop=False)
                    for h in halves:
                        last = nc.tensor.matmul(front[:, h], ident_bf[:, :], mask[:, h], start=False, stop=True)
                    last.then_inc(scores_done, 1)
                if g := group("yT"):
                    pe.wait_ge(y_copied, g.count(1, 1))
                    transposes(y_sb).then_inc(yT_done, 1)
                if g := group("Wh"):
                    pe.wait_ge(hT_ready, g.count(1, 1))
                    for cols in graphs:
                        last = nc.tensor.matmul(front[:, cols], hT[:, cols], Wg[:, :], start=True, stop=True)
                    last.then_inc(Wh_done, 1)
                if g := group("probsT"):
                    pe.wait_ge(exp_ready, g.count(1, 1))
                    transposes(probs).then_inc(probsT_done, 1)
                if g := group("attn"):
                    pe.wait_ge(probsT_ready, g.count(1, 1))
                    pe.wait_ge(Wh_ready, g.count(1, 1))
                    for cols in graphs:
                        last = nc.tensor.matmul(front[:, cols], probsT[:, cols], Wh[:, cols], start=True, stop=True)
                    last.then_inc(attn_done, 1)
                if g := group("cwT"):
                    pe.wait_ge(router_step, g.count(RT_STEPS, 14))
                    nc.tensor.transpose(front[:, 0:P], cw[:, :, :].rearrange("p e g -> p (e g)"), ident[:, :])\
                        .then_inc(cwT_done, 1)

            def iteration(i):
                for s in range(UNITS):
                    front_step(i, s, 0)
                    if unit := unit_at(i, s, 0):
                        up(*unit, unit[0].parity)
                    front_step(i, s, 1)
                    if unit := unit_at(i, s, LAG):
                        down(*unit)
                    front_step(i, s, 2)

            run_iterations(pe, NG, iteration)


_INS = ["x", "adj", "L0_gnn_W", "L0_gnn_a", "L0_ffn_gate_w", "L0_ffn_gate_b", "L0_ffn_W1", "L0_ffn_b1", "L0_ffn_W2",
        "L0_ffn_b2"]


def kernel(**inputs):
    import numpy as np
    import concourse.bacc as bacc
    from concourse.bass_utils import run_bass_kernel_spmd

    nc = bacc.Bacc("TRN2", target_bir_lowering=False, num_devices=1)
    arrays, args = {}, []
    for name in _INS:
        v = np.ascontiguousarray(inputs[name])
        arrays[f"in_{name}"] = v
        args.append(nc.dram_tensor(f"in_{name}", v.shape, mybir.dt.from_np(v.dtype), kind="ExternalInput").ap())
    out = nc.dram_tensor("out_x", inputs["x"].shape, F32, kind="ExternalOutput").ap()
    groups = inputs["x"].shape[0] // GB
    cw_dram = nc.dram_tensor("cw_dram", (groups, 2 * E, T), F32, kind="Internal").ap()
    build(nc, *args, out, cw_dram)
    r = run_bass_kernel_spmd(nc, [arrays], core_ids=[0])
    return r.results[0]["out_x"]
```
